# Optimizing a Trainium2 kernel written in Bass

```python
import numpy as np
import jax
import jax.numpy as jnp

def _softmax(x, axis=-1):
    return jax.nn.softmax(x, axis=axis)

def _gelu(x):
    return jax.nn.gelu(x, approximate=True)

def _silu(x):
    return jax.nn.silu(x)

def _sigmoid(x):
    return jax.nn.sigmoid(x)

def _layernorm(x, axis=-1, eps=1e-05):
    m = jnp.mean(x, axis=axis, keepdims=True)
    v = jnp.var(x, axis=axis, keepdims=True)
    return (x - m) / jnp.sqrt(v + eps)

def _scatter_add(tgt, idx, src, axis=0):
    return tgt.at[idx].add(src)

def _segment_sum(src, seg, n):
    return jax.ops.segment_sum(src, seg, n)
kernel_name = 'mk_flamingo_gated_d1_seqx_r4_f5d648'

def setup_inputs(seed: int=0):
    np.random.seed(seed)
    _w = jnp.asarray

    def _rec_inputs():
        import jax
        import jax.numpy as jnp
        _rk = jax.random.key(seed)
        x = -0.0002928 + 1 * jax.random.normal(jax.random.fold_in(_rk, 1), (4, 512, 256), jnp.float32)
        _lenS = 512 - jax.random.randint(jax.random.fold_in(_rk, 7), (4,), 0, max(1, 512 // 4) + 1, jnp.int32)
        _lenS2 = 512 - jax.random.randint(jax.random.fold_in(_rk, 8), (4,), 0, max(1, 512 // 4) + 1, jnp.int32)
        _ctx_2048P = jax.random.normal(jax.random.fold_in(_rk, 11), (4, 16, 512), jnp.float32)
        _ctx_2048c = jax.random.dirichlet(jax.random.fold_in(_rk, 511), 0.3 * jnp.ones((16,), jnp.float32), (4, 512))
        _ctx_2048t = jnp.einsum('bsk,bkd->bsd', _ctx_2048c, _ctx_2048P)
        _ctx_2048t = _ctx_2048t * jax.lax.rsqrt(jnp.mean(jnp.square(_ctx_2048t)) + 1e-12) * 0.953939
        ctx_2048 = -0.000514642 + 1.00011 * (_ctx_2048t + 0.3 * jax.random.normal(jax.random.fold_in(_rk, 611), (4, 512, 512), jnp.float32))
        _g = jax.random.normal(jax.random.fold_in(_rk, 9001), (2, 1), jnp.float32)
        _g = jnp.sign(_g) * jnp.maximum(jnp.abs(_g), 1.0) + (_g == 0) * 1.0
        g_xattn = _g[0]
        g_ffn = _g[1]
        return (x, ctx_2048, g_xattn, g_ffn)
    x, ctx_2048, g_xattn, g_ffn = _rec_inputs()

    def _L0_xattn_setup():
        import jax, jax.numpy as jnp
        import numpy as np
        NUM_HEADS = 16
        key = jax.random.key(seed)
        ks = jax.random.split(key, 5)
        dim = 256
        B, N, N_c = (4, 256, 64)
        x = jax.random.normal(ks[0], (B, N, dim), dtype=jnp.float32)
        context = jax.random.normal(ks[1], (B, N_c, 2 * dim), dtype=jnp.float32)
        w_qkv = jax.random.normal(ks[2], (3 * dim, dim), dtype=jnp.float32) * 0.02
        w_proj = jax.random.normal(ks[3], (dim, dim), dtype=jnp.float32) * 0.02
        b_proj = jax.random.normal(ks[4], (dim,), dtype=jnp.float32) * 0.02
        return {'x': x, 'context': context, 'w_qkv': w_qkv, 'w_proj': w_proj, 'b_proj': b_proj}
    _L0_xattn_all = _L0_xattn_setup()
    _L0_xattn_in = {k: v for k, v in _L0_xattn_all.items() if k in ('w_qkv', 'w_proj', 'b_proj')}
    del _L0_xattn_all

    def _L0_ffn_setup():
        import jax, jax.numpy as jnp
        import numpy as np
        NUM_EXPERTS = 8
        TOP_K = 2
        CAPACITY_FACTOR = 1.0

        def _dispatch_compute(xf, top_expert, w1, w2, capacity):
            tokens, hs = xf.shape
            tpe = jnp.bincount(top_expert, length=NUM_EXPERTS)
            indices = jnp.argsort(top_expert)
            offsets = jnp.concatenate([jnp.zeros((1,), tpe.dtype), jnp.cumsum(tpe)[:-1]])
            slot = jnp.arange(capacity)
            pos = offsets[:, None] + slot[None, :]
            valid = slot[None, :] < tpe[:, None]
            tok_idx = indices[jnp.minimum(pos, tokens - 1)]
            xe = jnp.where(valid[..., None], xf[tok_idx], 0.0)
            h = jax.nn.gelu(jnp.einsum('ech,ehf->ecf', xe, w1), approximate=True)
            ye = jnp.einsum('ecf,efh->ech', h, w2)
            tok_safe = jnp.where(valid, tok_idx, tokens)
            out = jnp.zeros((tokens + 1, hs), xf.dtype).at[tok_safe.reshape(-1)].add(ye.reshape(-1, hs))
            return out[:tokens]
        key = jax.random.key(seed)
        k1, k2, k3, k4 = jax.random.split(key, 4)
        hs, ffn = (256, 1024)
        x = jax.random.normal(k1, (512, 2, hs), dtype=jnp.float32)
        router_w = jax.random.normal(k2, (hs, NUM_EXPERTS), dtype=jnp.float32) * hs ** (-0.5)
        w1 = jax.random.normal(k3, (NUM_EXPERTS, hs, ffn), dtype=jnp.float32) * 0.02
        w2 = jax.random.normal(k4, (NUM_EXPERTS, ffn, hs), dtype=jnp.float32) * 0.02
        bias = jnp.zeros((1, 1, hs), dtype=jnp.float32)
        return {'x': x, 'router_w': router_w, 'w1': w1, 'w2': w2, 'bias': bias}
    _L0_ffn_all = _L0_ffn_setup()
    _L0_ffn_in = {k: v for k, v in _L0_ffn_all.items() if k in ('router_w', 'w1', 'w2', 'bias')}
    del _L0_ffn_all
    return {'x': x, 'ctx_2048': ctx_2048, 'g_xattn': g_xattn, 'g_ffn': g_ffn, 'L0_xattn_w_qkv': _L0_xattn_in['w_qkv'], 'L0_xattn_w_proj': _L0_xattn_in['w_proj'], 'L0_xattn_b_proj': _L0_xattn_in['b_proj'], 'L0_ffn_router_w': _L0_ffn_in['router_w'], 'L0_ffn_w1': _L0_ffn_in['w1'], 'L0_ffn_w2': _L0_ffn_in['w2'], 'L0_ffn_bias': _L0_ffn_in['bias']}

def reference(x, ctx_2048, g_xattn, g_ffn, L0_xattn_w_qkv, L0_xattn_w_proj, L0_xattn_b_proj, L0_ffn_router_w, L0_ffn_w1, L0_ffn_w2, L0_ffn_bias):
    import jax
    import jax.numpy as jnp

    def _L0_xattn_ref(x, context, w_qkv, w_proj, b_proj):
        import jax, jax.numpy as jnp
        import numpy as np
        NUM_HEADS = 16
        B, N, C = x.shape
        H = NUM_HEADS
        D = C // H
        scale = D ** (-0.5)
        qkv = (x @ w_qkv.T).reshape(B, N, 3, H, D).transpose(2, 0, 3, 1, 4)
        q, k, v = (qkv[0], qkv[1], qkv[2])
        N_c = context.shape[1]
        kv = context.reshape(B, N_c, 2, H, D).transpose(2, 0, 3, 1, 4)
        extra_k, extra_v = (kv[0], kv[1])
        k = jnp.concatenate([extra_k, k], axis=2)
        v = jnp.concatenate([extra_v, v], axis=2)
        dtype = q.dtype
        attn = jnp.einsum('bhnd,bhmd->bhnm', q * scale, k).astype(jnp.float32)
        attn = jax.nn.softmax(attn, axis=-1).astype(dtype)
        out = jnp.einsum('bhnm,bhmd->bhnd', attn, v)
        out = out.transpose(0, 2, 1, 3).reshape(B, N, C)
        return out @ w_proj.T + b_proj

    def _L0_ffn_ref(x, router_w, w1, w2, bias):
        import jax, jax.numpy as jnp
        import numpy as np
        NUM_EXPERTS = 8
        TOP_K = 2
        CAPACITY_FACTOR = 1.0

        def _dispatch_compute(xf, top_expert, w1, w2, capacity):
            tokens, hs = xf.shape
            tpe = jnp.bincount(top_expert, length=NUM_EXPERTS)
            indices = jnp.argsort(top_expert)
            offsets = jnp.concatenate([jnp.zeros((1,), tpe.dtype), jnp.cumsum(tpe)[:-1]])
            slot = jnp.arange(capacity)
            pos = offsets[:, None] + slot[None, :]
            valid = slot[None, :] < tpe[:, None]
            tok_idx = indices[jnp.minimum(pos, tokens - 1)]
            xe = jnp.where(valid[..., None], xf[tok_idx], 0.0)
            h = jax.nn.gelu(jnp.einsum('ech,ehf->ecf', xe, w1), approximate=True)
            ye = jnp.einsum('ecf,efh->ech', h, w2)
            tok_safe = jnp.where(valid, tok_idx, tokens)
            out = jnp.zeros((tokens + 1, hs), xf.dtype).at[tok_safe.reshape(-1)].add(ye.reshape(-1, hs))
            return out[:tokens]
        sl, bs, hs = x.shape
        tokens = sl * bs
        capacity = int(CAPACITY_FACTOR * tokens / NUM_EXPERTS)
        xf = x.reshape(tokens, hs)
        scores = jax.nn.softmax(xf @ router_w, axis=-1)
        expert_weights, top_experts = jax.lax.top_k(scores, TOP_K)
        out = jnp.zeros_like(xf)
        for k in range(TOP_K):
            y = _dispatch_compute(xf, top_experts[:, k].astype(jnp.int32), w1, w2, capacity)
            out = out + y * expert_weights[:, k][:, None]
        return out.reshape(sl, bs, hs) + bias
    x = x + jnp.tanh(g_xattn[0]) * _L0_xattn_ref(_layernorm(x, axis=-1), ctx_2048, L0_xattn_w_qkv, L0_xattn_w_proj, L0_xattn_b_proj)
    x = x + jnp.tanh(g_ffn[0]) * _L0_ffn_ref(_layernorm(x, axis=-1), L0_ffn_router_w, L0_ffn_w1, L0_ffn_w2, L0_ffn_bias)
    return x

_drawn_inputs = setup_inputs


def setup_inputs(seed=0):
    import zlib

    import numpy as np

    out = dict(_drawn_inputs(seed))
    spreads = {'L0_ffn_bias': (0.0, 0.1)}
    factors = {'L0_xattn_w_qkv': 6.145, 'L0_xattn_b_proj': 3.737, 'ctx_2048': 4.678}
    for name, (base, spread) in spreads.items():
        noise = np.random.default_rng([zlib.crc32(name.encode()), seed]).standard_normal(out[name].shape)
        drawn = base * np.exp(spread * noise) if base else spread * noise
        out[name] = jnp.asarray(drawn.astype(out[name].dtype))
    for name, factor in factors.items():
        out[name] = (out[name] * factor).astype(out[name].dtype)
    return out
```

```python
from contextlib import ExitStack

import concourse.bass as bass
from concourse import mybir

ALU = mybir.AluOpType
ACT = mybir.ActivationFunctionType
F32 = mybir.dt.float32
F32R = mybir.dt.float32r
BF16 = mybir.dt.bfloat16
U32 = mybir.dt.uint32
I32 = mybir.dt.int32
AX_X = mybir.AxisListType.X

P = 128
B, T, C = 4, 512, 256
H, D = 16, 16
TC = 512
NKEY = TC + T
KT = NKEY // P
QT = T // P
G, HG = 4, 4
NGROUP = B * G
E, F, TOPK = 8, 1024, 2
NTOK = B * T
CAP = NTOK // E
SLOTS = TOPK * CAP
NSLOT = E * SLOTS
ROW = C + TOPK + 1
NPART = 3
PAIRS = [(0, 0), (0, 1), (0, 2), (1, 0), (1, 1), (2, 0)]
KROWS = len(PAIRS) * D
AROWS = KROWS + NPART
EPS = 1e-5
ROOT_SEED = 1597463007.0
NEWTON = 3
NORM_LINKS = 6 + 3 * NEWTON
NOBODY = 1 << 20
DROPPED = 1 << 16

SLOTS_PER_GROUP = 16
STEPS = NGROUP * SLOTS_PER_GROUP
PERIOD = G * SLOTS_PER_GROUP
LEAD = 24
TURN = PERIOD - LEAD
NP = 4


def steps_at(c):
    s, p, g = c % SLOTS_PER_GROUP, c % PERIOD, c // SLOTS_PER_GROUP
    behind = 1 <= g <= NGROUP
    if c + LEAD < STEPS:
        yield "max", c + LEAD
    if c < STEPS:
        yield "scores", c
    if behind and s == 1:
        yield "values", KT - 1
    if c < STEPS and s % 2 and s >= 3:
        yield "values", (s - 3) // 2
    if behind and s == 1 and g + 3 < NGROUP:
        yield "load", g + 3
    if behind and s == 2:
        yield "copy_out", g - 1
    if s == 2 and g >= 3 and g + 1 < NGROUP:
        yield "set_v", g + 1
    if behind and s == 5:
        yield "turn_out", g - 1
    if s == 10 and g + 1 < NGROUP:
        yield "turn_max", g + 1
    for name in ROUTE_AT.get(p, []) if c >= PERIOD else []:
        yield name, c // PERIOD - 1


ROUTE_AT = {8: ["attn_t0"], 9: ["attn_t1"], 12: ["proj0"], 13: ["proj1"], 14: ["norm2"],
            20: ["x1_t0"], 21: ["x1_t1"], 24: ["router"], 26: ["top2"], 36: ["ranks"], 39: ["scatter"]}
SHARED = ("turn_out", "turn_max", "attn_t0", "attn_t1", "proj0", "proj1", "x1_t0", "x1_t1", "router",
          "ranks")
TURNS = 2 * G + 8


class Tally:

    def __init__(self):
        self.n, self.reg, self.per = 0, None, 0

    def step(self, m=1):
        self.n += m

    def at(self, d=0):
        return self.n + d if self.reg is None else self.reg * self.per + (self.n + d)

    def begin(self, reg, per):
        self.reg, self.per, self.n0 = reg, per, self.n

    def end(self, turns):
        assert self.n - self.n0 == self.per, (self.n - self.n0, self.per)
        self.n, self.reg = self.n0 + self.per * turns, None


def build(nc, x_in, ctx_kT, ctx_v, g_x, g_f, w_qkvT, w_projT, b_proj, router_w, w1, w2, bias, out):
    stack = ExitStack()
    phase1 = ExitStack()
    phase2 = ExitStack()

    def sb(name, shape, dt, where=stack):
        return where.enter_context(nc.sbuf_tensor(name, shape, dt))

    def sem(name):
        return stack.enter_context(nc.semaphore(name))

    with stack:
        ident = sb("ident", [P, P], F32)
        below = sb("below", [P, P], BF16)
        ones = sb("ones", [P, P], BF16)
        iota_e = sb("iota_e", [P, E], F32)
        slot_base = sb("slot_base", [P, TOPK, E], F32)
        token_no = sb("token_no", [P, B * QT], F32)
        gates = sb("gates", [P, 2], F32)
        tanh_g = sb("tanh_g", [P, 2], F32)
        b_row = sb("b_row", [P, C], F32)
        bias_row = sb("bias_row", [P, C], F32)
        x_sb = sb("x_sb", [P, B * QT, C], F32)
        w1_raw = [sb("w1_raw0", [P, 2, F], F32)]
        w2_raw = [sb("w2_raw0", [P, F // P, C], F32)]
        stats = sb("stats", [P, QT, 6], F32)
        meanvar = sb("meanvar", [P, QT, 2], F32)
        rstd = sb("rstd", [P, QT], F32)
        var = sb("var", [P, QT], F32)
        held_p = sb("held_p", [P, 10], F32)
        held = sb("held", [P, 2], F32)
        root_t = sb("root_t", [P, QT], F32)

        v_stash = sb("v_stash", [P, 2, B, QT, C], F32, phase1)
        v_ones = sb("v_ones", [P, KT, H, 2 * D], F32, phase1)
        q6 = sb("q6", [P, H, T], BF16, phase1)
        k6 = sb("k6", [P, H, NKEY], BF16, phase1)
        o_t = sb("o_t", [P, T], F32, phase1)
        o_nat = sb("o_nat", [P, QT, C], F32, phase1)
        o_natT = sb("o_natT", [P, 2, T], F32, phase1)
        w_p = sb("w_p", [P, 2, C], F32, phase1)
        w_r = sb("w_r", [P, 2, E], F32, phase1)
        xd = sb("xd", [P, QT, ROW], F32, phase1)
        x1T = sb("x1T", [P, 2, T], F32, phase1)
        rden = sb("rden", [P, QT, HG], F32, phase1)
        mx = sb("mx", [P, 2, SLOTS_PER_GROUP], F32, phase1)
        neg_m = sb("neg_m", [SLOTS_PER_GROUP, P], F32, phase1)
        neg_parts = sb("neg_parts", [SLOTS_PER_GROUP, NPART, P], BF16, phase1)
        lmax = sb("lmax", [P, QT], F32, phase1)
        lshift = sb("lshift", [P, QT, E], F32, phase1)
        lexp = sb("lexp", [P, QT, E], F32, phase1)
        lsum = sb("lsum", [P, QT], F32, phase1)
        score = sb("score", [P, QT, E], F32, phase1)
        top = sb("top", [P, QT, 8], F32, phase1)
        top_e = sb("top_e", [P, QT, 8], U32, phase1)
        top_ef = sb("top_ef", [P, QT, TOPK], F32, phase1)
        hot = sb("hot", [P, QT, TOPK * E], BF16, phase1)
        hot_sum = sb("hot_sum", [P, TOPK * E], F32, phase1)
        carry = sb("carry", [P, TOPK * E], BF16, phase1)
        pos = sb("pos", [P, QT, TOPK * E], F32, phase1)
        over = sb("over", [P, QT, TOPK * E], F32, phase1)
        slot_f = sb("slot_f", [P, QT, TOPK], F32, phase1)
        slot_u = sb("slot_u", [P, QT, TOPK], U32, phase1)
        parts = sb("parts", [P, NPART, 4, T], BF16, phase1)
        c_parts = sb("c_parts", [P, NPART, 2, T], BF16, phase1)
        empty = sb("empty", [P, ROW], F32, phase1)
        with ExitStack() as early:
            xn = sb("xn", [P, QT, C], F32, early)
            xnT = sb("xnT", [P, 2, T], F32, early)
            w_qkv = sb("w_qkv", [P, 2, 3 * C], F32, early)
            qk = sb("qk", [P, 4, T], F32, early)
            ctxk = sb("ctxk", [P, 2, T], F32, early)
        pexp = [sb(f"pexp{i}", [P, HG, T], F32, phase1) for i in range(NP)]
        phase1.close()

        w1_raw.append(sb("w1_raw1", [P, 2, F], F32, phase2))
        w2_raw.append(sb("w2_raw1", [P, F // P, C], F32, phase2))
        xe = [sb(f"xe{i}", [P, SLOTS // P, ROW], F32, phase2) for i in range(2)]
        tok_u = [sb(f"tok_u{i}", [P, SLOTS // P], U32, phase2) for i in range(2)]
        xeT = [sb(f"xeT_{h}", [P, 2, SLOTS], F32R, phase2) for h in ("hi", "lo")]
        w1_p = [[sb(f"w1_{h}{i}", [P, 2, F], F32R, phase2) for h in ("hi", "lo")] for i in range(2)]
        w2_p = [[sb(f"w2_{h}{i}", [P, F // P, C], F32R, phase2) for h in ("hi", "lo")] for i in range(2)]
        hid = sb("hid", [P, 4, SLOTS], F32, phase2)
        hid_p = [sb(f"hid_{h}", [P, F // P, SLOTS], F32R, phase2) for h in ("hi", "lo")]
        y_sb = [sb(f"y_sb{i}", [P, SLOTS // P, C], F32, phase2) for i in range(2)]
        phase2.close()

        ps = stack.enter_context(nc.psum_tensor("ps", [P, 8, 512], F32))

        q_dram = nc.dram_tensor("q_parts", (B, NPART, C, T), BF16, kind="Internal").ap()
        k_dram = nc.dram_tensor("k_parts", (B, NPART, C, NKEY), BF16, kind="Internal").ap()
        slot_dram = nc.dram_tensor("slot_rows", (NSLOT, ROW), F32, kind="Internal").ap()

        chain_v, chain_p = sem("chain_v"), sem("chain_p")
        consts_in, x_in_s, w_in, vctx_in, ctxk_in = (sem(n) for n in (
            "consts_in", "x_loaded", "w_loaded", "vctx_loaded", "ctxk_loaded"))
        gate_in, gates_done = sem("gates_loaded"), sem("gates_done")
        consts_done, empty_done, empty_out = sem("consts_done"), sem("empty_done"), sem("empty_out")
        xn_done, xnT_ready, xnT_done = sem("xn_done"), sem("xnT_ready"), sem("xnT_done")
        qkv_ready, qkv_out = sem("qkv_ready"), sem("qkv_out")
        parts_done, cparts_done = sem("parts_done"), sem("cparts_done")
        parts_out, cparts_out = sem("parts_stored"), sem("cparts_stored")
        xb_done = sem("xb_done")
        one_row, k_ones = sem("one_row"), sem("k_ones")
        qk_in = [sem(f"qk_loaded{g}") for g in range(G)]
        shift_in = [sem(f"shift_in{g}") for g in range(G)]
        s_ready, max_done = sem("max_scores_ready"), sem("max_done")
        st_ready, exp_done = sem("scores_ready"), sem("exp_done")
        pv_done, o_copied = sem("pv_done"), sem("o_copied")
        v_set = sem("v_set")
        misc_ready, misc_free = sem("misc_ready"), sem("misc_free")
        shift_done = sem("shift_parts_done")
        x1_done, xd_done = sem("x1_done"), sem("xd_done")
        lexp_done, hot_done, slot_done = sem("lexp_done"), sem("hot_done"), sem("slot_done")
        res_done, res_out, scattered = sem("residual_done"), sem("residual_stored"), sem("scattered")
        w_raw_in = [sem(f"w_raw_in{i}") for i in range(2)]
        xe_in = [sem(f"xe_in{i}") for i in range(2)]
        xeT_ready, xeT_done = sem("xeT_ready"), sem("xeT_done")
        w_cut = sem("w_cut")
        h_ready, h_out, hid_done = sem("h_ready"), sem("h_out"), sem("hid_done")
        hhi_done, y_ready, y_done = sem("hhi_done"), sem("y_ready"), sem("y_done")
        tok_done, added, rows_added = sem("tok_done"), sem("added"), sem("rows_added")
        xd_free = sem("xd_free")

        def bank(i, n=1):
            return ps[:, i, :] if n == 1 else ps[:, i:i + n, :]

        MISC = bank(7)
        SPE = SLOTS // P
        FT = F // P

        def run_steps(eng, steps, tallies, turn=TURN):
            steps(0, turn)
            with eng.Fori(0, B - 1) as i:
                for t, per in tallies:
                    t.begin(i, per)
                steps(turn, turn + PERIOD, i)
                for t, per in tallies:
                    t.end(B - 1)
            steps(turn + PERIOD * (B - 1), STEPS + PERIOD)

        block = stack.enter_context(nc.Block())

        @block.sync
        def _(sp):
            sp.sem_inc(parts_out, 6 * 16)
            sp.dma_start(gates[:, 0:1], g_x.broadcast_to([P, 1])).then_inc(gate_in, 16)
            sp.dma_start(gates[:, 1:2], g_f.broadcast_to([P, 1])).then_inc(gate_in, 16)
            sp.dma_start(x_sb[:, :, :], x_in.rearrange("(t p) c -> p t c", p=P)).then_inc(x_in_s, 16)
            sp.dma_start(w_qkv[:, :, :], w_qkvT.rearrange("(k p) n -> p k n", p=P)).then_inc(w_in, 16)
            sp.dma_start(b_row[:, :], b_proj.broadcast_to([P, C])).then_inc(consts_in, 16)
            sp.dma_start(bias_row[:, :], bias.broadcast_to([P, C])).then_inc(consts_in, 16)
            sp.dma_start(w_p[:, :, :], w_projT.rearrange("(k p) n -> p k n", p=P)).then_inc(consts_in, 16)
            sp.dma_start(w_r[:, :, :], router_w.rearrange("(k p) n -> p k n", p=P)).then_inc(consts_in, 16)
            sp.dma_start(v_stash[:, 0, :, :, :].rearrange("p b t c -> p (b t) c"),
                         ctx_v.rearrange("b (t p) c -> p (b t) c", p=P)).then_inc(vctx_in, 16)
            sp.wait_ge(one_row, 1)
            sp.dma_start(k6[KROWS:AROWS, 1:H, :], k6[KROWS:AROWS, 0:1, :].to_broadcast([NPART, H - 1, NKEY])) \
                .then_inc(k_ones, 16)
            with sp.Fori(0, B) as b:
                sp.wait_ge(cparts_done, b + 1)
                sp.dma_start(ctxk[:, :, :], ctx_kT[bass.ds(b, 1)].rearrange("a (m p) t -> p (a m) t", p=P)) \
                    .then_inc(ctxk_in, 16)
                sp.wait_ge(cparts_done, b + 2)
                for i in range(NPART):
                    sp.dma_start(k_dram[bass.ds(b, 1), i, :, 0:TC].rearrange("a (m p) t -> p (a m) t", p=P),
                                 c_parts[:, i, :, :]).then_inc(cparts_out, 16)
                sp.wait_ge(parts_done, b + 2)
                for i in range(NPART):
                    sp.dma_start(q_dram[bass.ds(b, 1), i].rearrange("a (m p) t -> p (a m) t", p=P),
                                 parts[:, i, 0:2, :]).then_inc(parts_out, 16)
                    sp.dma_start(k_dram[bass.ds(b, 1), i, :, TC:NKEY].rearrange("a (m p) t -> p (a m) t", p=P),
                                 parts[:, i, 2:4, :]).then_inc(parts_out, 16)

            def load_weights(e, k):
                sp.dma_start(w1_raw[k][:, :, :], w1[bass.ds(e, 1)].rearrange("a (k p) f -> p (a k) f", p=P)) \
                    .then_inc(w_raw_in[k], 16)
                sp.dma_start(w2_raw[k][:, :, :], w2[bass.ds(e, 1)].rearrange("a (k p) c -> p (a k) c", p=P)) \
                    .then_inc(w_raw_in[k], 16)

            def load_rows(e, k):
                sp.dma_start(xe[k][:, :, :], slot_dram[bass.ds(e * SLOTS, SLOTS), :]
                             .rearrange("(s p) c -> p s c", p=P)).then_inc(xe_in[k], 16)

            def load_group(b, g):
                for r, (pq, pk) in enumerate(PAIRS):
                    sp.dma_start(q6[r * D:(r + 1) * D, HG * g:HG * (g + 1), :],
                                 q_dram[bass.ds(b, 1), pq, HG * D * g:HG * D * (g + 1), :]
                                 .rearrange("a (h d) t -> d (a h) t", d=D)).then_inc(qk_in[g], 16)
                    sp.dma_start(k6[r * D:(r + 1) * D, HG * g:HG * (g + 1), :],
                                 k_dram[bass.ds(b, 1), pk, HG * D * g:HG * D * (g + 1), :]
                                 .rearrange("a (h d) t -> d (a h) t", d=D)).then_inc(qk_in[g], 16)

            sp.wait_ge(parts_out, 6 * 16 * (B + 1))
            sp.wait_ge(cparts_out, 3 * 16 * (B + 1))
            for g in range(G):
                load_group(0, g)
            sp.wait_ge(empty_done, 1)
            sp.dma_start(slot_dram.rearrange("(n p) c -> p n c", p=P),
                         empty[:, :].rearrange("p (o c) -> p o c", o=1).to_broadcast([P, NSLOT // P, ROW])) \
                .then_inc(empty_out, 16)
            load_weights(0, 0)

            st, shifts = Tally(), Tally()

            def shift_rows(g):
                shifts.step()
                sp.wait_ge(shift_done, shifts.at())
                for i in range(NPART):
                    sp.dma_start(q6[KROWS + i:KROWS + i + 1, HG * g:HG * (g + 1), :]
                                 .rearrange("o h (q t) -> o (h q) t", t=P),
                                 neg_parts[:, i, :]).then_inc(shift_in[g], 16)

            def steps(c0, c1, i=0):
                for c in range(c0, c1):
                    for what, n in steps_at(c):
                        if what == "scores":
                            st.step(2)
                        elif what == "load":
                            sp.wait_ge(st_ready, st.at(-4))
                            load_group(i + n // G, n % G)
                        elif what == "turn_max":
                            shift_rows(n % G)

            shift_rows(0)
            run_steps(sp, steps, [(st, 2 * PERIOD), (shifts, G)], turn=2)

            sp.wait_ge(pv_done, NGROUP * KT)
            sp.wait_ge(scattered, B * QT * TOPK * 16)
            sp.wait_ge(res_out, B * 16)
            load_rows(0, 0)
            load_weights(1, 1)
            load_rows(1, 1)

            def reload(n, k):
                sp.wait_ge(w_cut, n + 1)
                load_weights(n + 2, k)
                sp.wait_ge(y_done, (n + 1) * SPE + 2)
                load_rows(n + 2, k)

            with sp.Fori(0, (E - 2) // 2) as j:
                reload(j * 2, 0)
                reload(j * 2 + 1, 1)
            sp.wait_ge(added, E * SPE * 16)

        @block.gpsimd
        def _(pool):
            link_n = Tally()

            def link(ins):
                ins.then_inc(chain_p, 1)
                link_n.step()
                pool.wait_ge(chain_p, link_n.at())

            def touch(k):
                return pool.tensor_tensor(held_p[:, k:k + 1], held_p[:, 9:10], held_p[:, 9:10], ALU.mult)

            def hold(k):
                touch(k).then_inc(chain_p, 1)
                link_n.step()

            def copy(dst, src):
                names = {2: "p (a) -> p a", 3: "p (a b) -> p a b", 4: "p (a b c) -> p a b c"}[len(src.shape)]
                units = {k: 1 for k in "abc"[:len(src.shape) - 2]}
                one = held_p[0:src.shape[0], 9:10].rearrange(names, **units)
                return pool.tensor_tensor(dst, src, one.to_broadcast(list(src.shape)), ALU.mult)

            def spread(row, n):
                return row[:, :].rearrange("p (o c) -> p o c", o=1).to_broadcast([P, n, C])

            pool.sem_inc(cparts_done, 1)
            pool.sem_inc(cparts_out, 3 * 16)
            pool.sem_inc(xd_free, 1)
            pool.sem_inc(rows_added, 2)
            link(pool.memset(held_p[:, 9:10], 1.0))
            link(pool.memset(ident[:, :], 0.0))
            pool.affine_select(out=ident[:, :], in_=ident[:, :], compare_op=ALU.not_equal, fill=1.0, base=0,
                               pattern=[[-1, P]], channel_multiplier=1).then_inc(consts_done, 1)

            link(pool.memset(ones[:, :], 1.0))
            pool.affine_select(out=below[:, :], in_=ones[:, :], compare_op=ALU.is_gt, fill=0.0, base=0,
                               pattern=[[1, P]], channel_multiplier=-1)
            pool.iota(iota_e[:, :], pattern=[[1, E]], base=0, channel_multiplier=0,
                      allow_small_or_imprecise_dtypes=True)
            pool.iota(slot_base[:, :, :], pattern=[[CAP, TOPK], [SLOTS, E]], base=0, channel_multiplier=0,
                      allow_small_or_imprecise_dtypes=True)
            pool.iota(token_no[:, :], pattern=[[P, B * QT]], base=0, channel_multiplier=1,
                      allow_small_or_imprecise_dtypes=True)
            pool.memset(carry[:, :], 0.0)
            link(pool.memset(empty[:, :], 0.0))
            pool.memset(empty[:, C + TOPK:ROW], float(NOBODY)).then_inc(empty_done, 1)

            def batch(b):
                pool.wait_ge(ctxk_in, (b + 1) * 16)
                pool.wait_ge(cparts_out, (b + 1) * (3 * 16))
                link(copy(c_parts[:, 0], ctxk[:, :, :]))
                link(pool.tensor_tensor(ctxk[:, :, :], ctxk[:, :, :], c_parts[:, 0], ALU.subtract))
                link(copy(c_parts[:, 1], ctxk[:, :, :]))
                pool.tensor_tensor(c_parts[:, 2], ctxk[:, :, :], c_parts[:, 1], ALU.subtract) \
                    .then_inc(cparts_done, 1)

            with pool.Fori(0, B - 1) as b:
                link_n.begin(b, 3)
                batch(b)
                link_n.end(B - 1)
            batch(B - 1)
            pool.memset(v_ones[:, :, :, D:2 * D], 1.0).then_inc(consts_done, 1)
            pool.wait_ge(vctx_in, 16)
            pool.wait_ge(qkv_out, 6 * (B + 1))

            pv, turn, rt = Tally(), Tally(), Tally()

            def set_v(b, g):
                for half in range(2):
                    ins = copy(
                        v_ones[:, half * QT:(half + 1) * QT, HG * g:HG * (g + 1), 0:D],
                        v_stash[:, half, bass.ds(b, 1), :, HG * D * g:HG * D * (g + 1)]
                        .rearrange("p o t (h d) -> p (o t) h d", d=D))
                ins.then_inc(v_set, 1)

            for g in range(G):
                set_v(0, g)

            def cut_max():
                pool.wait_ge(misc_free, turn.at())
                link(copy(neg_parts[:, 0, :], neg_m[:, :]))
                link(pool.tensor_tensor(neg_m[:, :], neg_m[:, :], neg_parts[:, 0, :], ALU.subtract))
                link(copy(neg_parts[:, 1, :], neg_m[:, :]))
                pool.tensor_tensor(neg_parts[:, 2, :], neg_m[:, :], neg_parts[:, 1, :], ALU.subtract) \
                    .then_inc(shift_done, 1)

            turn.step()
            cut_max()
            pool.wait_ge(gates_done, 1)
            pool.wait_ge(consts_in, 4 * 16)
            pool.tensor_scalar(bias_row[:, :], bias_row[:, :], tanh_g[:, 1:2], None, ALU.mult)
            link(pool.tensor_scalar(b_row[:, :], b_row[:, :], tanh_g[:, 0:1], None, ALU.mult))
            pool.wait_ge(xn_done, B)
            pool.tensor_tensor(x_sb[:, :, :], x_sb[:, :, :], spread(b_row, B * QT), ALU.add).then_inc(xb_done, 1)

            def steps(c0, c1, i=0):
                for c in range(c0, c1):
                    for what, n in steps_at(c):
                        if what in SHARED:
                            turn.step()
                        if what == "values":
                            pv.step()
                        elif what == "set_v":
                            pool.wait_ge(pv_done, pv.at(1 - 3 * KT))
                            set_v(i + n // G, n % G)
                        elif what == "turn_max":
                            pool.wait_ge(shift_in[(n - 1) % G], (i + ((n - 1) // G + 1)) * (16 * NPART))
                            cut_max()
                        elif what == "scatter":
                            rt.step()
                            pool.wait_ge(xd_done, rt.at())
                            rows = x_sb[:, bass.ds(i * QT + n * QT, QT), :]
                            pool.tensor_tensor(rows, rows, spread(bias_row, QT), ALU.add).then_inc(res_done, 1)
                            pool.wait_ge(empty_out, 16)
                            pool.wait_ge(slot_done, rt.at())
                            hold(0)
                            for t in range(QT):
                                for k in range(TOPK):
                                    pool.indirect_dma_start(
                                        out=slot_dram, out_offset=bass.IndirectOffsetOnAxis(
                                            ap=slot_u[:, t, k:k + 1], axis=0),
                                        in_=xd[:, t, :], in_offset=None,
                                        bounds_check=NSLOT - 1, oob_is_err=False).then_inc(scattered, 16)
                            pool.wait_ge(res_done, rt.at())
                            hold(1)
                            pool.dma_start(out[bass.ds(i * T + n * T, T), :].rearrange("(q p) c -> p q c", p=P),
                                           rows).then_inc(res_out, 16)
                            pool.wait_ge(scattered, rt.at() * (QT * TOPK * 16))
                            touch(2).then_inc(xd_free, 1)

            run_steps(pool, steps, [(pv, G * KT), (turn, TURNS), (rt, 1), (link_n, 3 * G + 2)])

            def add_rows(n, k):
                pool.wait_ge(tok_done, n + 1)
                link(touch(8))
                for s in range(SPE):
                    pool.wait_ge(y_done, n * SPE + (s + 3))
                    hold(3 + s)
                    pool.indirect_dma_start(
                        out=out, out_offset=bass.IndirectOffsetOnAxis(ap=tok_u[k][:, s:s + 1], axis=0),
                        in_=y_sb[k][:, s, :], in_offset=None, bounds_check=NTOK - 1, oob_is_err=False,
                        compute_op=ALU.add).then_inc(added, 16)
                pool.wait_ge(added, n * (SPE * 16) + SPE * 16)
                touch(7).then_inc(rows_added, 1)

            pool.wait_ge(res_out, B * 16)
            with pool.Fori(0, E // 2) as j:
                link_n.begin(j, 2 * (SPE + 1))
                add_rows(j * 2, 0)
                add_rows(j * 2 + 1, 1)
                link_n.end(E // 2)

        @block.scalar
        def _(act):
            act.sem_inc(qkv_out, 6)
            act.sem_inc(xnT_done, 2)
            act.sem_inc(h_out, 4)
            act.wait_ge(gate_in, 32)
            act.activation(tanh_g[:, :], gates[:, :], ACT.Tanh).then_inc(gates_done, 1)
            with act.Fori(0, B) as b:
                for k in range(2):
                    act.wait_ge(xnT_ready, b * 2 + (k + 1))
                    act.activation(xnT[:, k, :], bank(k), ACT.Copy).then_inc(xnT_done, 1)
                act.wait_ge(parts_done, b + 1)
                for m in range(4):
                    act.wait_ge(qkv_ready, b * 6 + (m + 1))
                    act.activation(qk[:, m, :], bank(2 + m), ACT.Copy, scale=D ** -0.5 if m < 2 else 1.0) \
                        .then_inc(qkv_out, 1)
                for j in range(2):
                    act.wait_ge(qkv_ready, b * 6 + (5 + j))
                    act.activation(v_stash[:, 1, bass.ds(b, 1), 2 * j:2 * j + 2, :].rearrange("p o t c -> p (o t c)"),
                                   bank(6 + j), ACT.Copy).then_inc(qkv_out, 1)

            st, kt_n, turn, oc, rt, tmax = (Tally() for _ in range(6))

            def evict(dst, scale=1.0, src=MISC):
                turn.step()
                act.wait_ge(misc_ready, turn.at())
                return act.activation(dst, src, ACT.Copy, scale=scale).then_inc(misc_free, 1)

            def turn_max():
                tmax.step()
                evict(neg_m[:, :], -1.0, MISC[0:SLOTS_PER_GROUP, 0:P])

            def steps(c0, c1, i=0):
                for c in range(c0, c1):
                    for what, n in steps_at(c):
                        if what == "scores":
                            kt, pair = c % SLOTS_PER_GROUP // 2, c % 2
                            buf = pexp[kt % NP]
                            if pair == 0:
                                kt_n.step()
                                if c >= 2 * NP:
                                    act.wait_ge(pv_done, kt_n.at(-NP))
                            for j in range(2):
                                st.step()
                                act.wait_ge(st_ready, st.at())
                                act.activation(buf[:, 2 * pair + j, :], bank(4 + j), ACT.Exp).then_inc(exp_done, 1)
                        elif what == "copy_out":
                            oc.step()
                            act.wait_ge(pv_done, oc.at() * KT)
                            act.wait_ge(misc_ready, turn.at())
                            act.activation(o_t[:, :], bank(6), ACT.Copy).then_inc(o_copied, 1)
                        elif what == "turn_max":
                            act.wait_ge(shift_done, tmax.at())
                            turn_max()
                        elif what in ("attn_t0", "attn_t1"):
                            evict(o_natT[:, int(what[-1]), :])
                        elif what in ("x1_t0", "x1_t1"):
                            evict(x1T[:, int(what[-1]), :])
                        elif what in SHARED:
                            turn.step()
                        elif what == "top2":
                            rt.step()
                            act.wait_ge(misc_free, turn.at())
                            act.activation(lexp[:, :, :], lshift[:, :, :], ACT.Exp).then_inc(lexp_done, 1)

            turn_max()
            act.wait_ge(parts_done, B + 1)
            act.wait_ge(cparts_done, B + 1)
            run_steps(act, steps, [(st, 2 * PERIOD), (kt_n, G * KT), (turn, TURNS), (oc, G), (rt, 1), (tmax, G)])

            with act.Fori(0, E) as e:
                for f in range(FT):
                    act.wait_ge(h_ready, e * FT + (f + 1))
                    act.wait_ge(hid_done, e * FT + (f + 1))
                    act.activation(hid[:, f % 4, :], bank(2 + f % 4), ACT.Gelu_apprx_tanh).then_inc(h_out, 1)
                    act.wait_ge(h_out, e * FT + (f + 5))
                    act.activation(hid_p[0][:, f, :], hid[:, f % 4, :], ACT.Copy).then_inc(hhi_done, 1)

        @block.vector
        def _(dve):
            link_n = Tally()

            def link(ins):
                ins.then_inc(chain_v, 1)
                link_n.step()
                dve.wait_ge(chain_v, link_n.at())

            def hold():
                dve.tensor_copy(held[:, 0:1], held[:, 1:2]).then_inc(chain_v, 1)
                link_n.step()

            def x_row(b, t):
                return x_sb[:, bass.ds(b * QT + t, 1), :].rearrange("p o c -> p (o c)")

            def layer_norm(dst, b, done):
                hold()
                for t in range(QT):
                    ins = dve.bn_stats(stats[:, t, :], x_row(b, t))
                link(ins)
                hold()
                for t in range(QT):
                    ins = dve.bn_aggr(meanvar[:, t, :], stats[:, t, :])
                link(ins)
                link(dve.tensor_scalar(var[:, :], meanvar[:, :, 1], EPS, None, ALU.add))
                link(dve.tensor_scalar(rstd[:, :].bitcast(I32), var[:, :].bitcast(I32), -0.5, ROOT_SEED,
                                       ALU.mult, ALU.add))
                for _ in range(NEWTON):
                    link(dve.scalar_tensor_tensor(out=root_t[:, :], in0=rstd[:, :], scalar=-0.5, in1=rstd[:, :],
                                                  op0=ALU.mult, op1=ALU.mult))
                    link(dve.tensor_tensor(root_t[:, :], root_t[:, :], var[:, :], ALU.mult))
                    link(dve.scalar_tensor_tensor(out=rstd[:, :], in0=root_t[:, :], scalar=1.5, in1=rstd[:, :],
                                                  op0=ALU.add, op1=ALU.mult))
                for t in range(QT):
                    ins = dve.tensor_scalar(dst[:, t, 0:C], x_row(b, t), meanvar[:, t, 0:1],
                                            rstd[:, t:t + 1], ALU.subtract, ALU.mult)
                ins.then_inc(done, 1)

            def cut(b):
                dve.wait_ge(qkv_out, b * 6 + 10)
                dve.wait_ge(parts_out, (b + 1) * (6 * 16))
                link(dve.tensor_copy(parts[:, 0], qk[:, :, :]))
                link(dve.tensor_tensor(qk[:, :, :], qk[:, :, :], parts[:, 0], ALU.subtract))
                link(dve.tensor_copy(parts[:, 1], qk[:, :, :]))
                dve.tensor_tensor(parts[:, 2], qk[:, :, :], parts[:, 1], ALU.subtract).then_inc(parts_done, 1)

            dve.sem_inc(parts_done, 1)
            dve.sem_inc(hid_done, 4)
            dve.sem_inc(y_done, 2)
            dve.memset(k6[KROWS:P, 0:1, :], 1.0).then_inc(one_row, 1)
            link(dve.memset(held[:, :], 0.0))
            dve.wait_ge(x_in_s, 16)
            layer_norm(xn, 0, xn_done)
            with dve.Fori(0, B - 1) as b:
                link_n.begin(b, NORM_LINKS + 3)
                dve.wait_ge(xnT_ready, (b + 1) * 2)
                layer_norm(xn, b + 1, xn_done)
                cut(b)
                link_n.end(B - 1)
            cut(B - 1)

            unit, turn, rt = Tally(), Tally(), Tally()

            def row_max(u):
                unit.step()
                dve.wait_ge(s_ready, unit.at())
                group, j = u // SLOTS_PER_GROUP, u % SLOTS_PER_GROUP
                dve.reduce_max(mx[:, group % 2, j:j + 1], bank(2 * (u % 2), 2).rearrange("p a t -> p (a t)"),
                               AX_X).then_inc(max_done, 1)

            def wait_turn():
                turn.step()
                dve.wait_ge(misc_ready, turn.at())

            def per_row(x, n, shape):
                return x.rearrange("p (q o) -> p q o", o=1).to_broadcast(shape)

            def steps(c0, c1, i=0):
                for c in range(c0, c1):
                    for what, n in steps_at(c):
                        if what == "max":
                            row_max(n)
                        elif what == "turn_out":
                            wait_turn()
                            o4 = MISC.rearrange("p (q h d) -> p q h d", q=QT, h=HG)
                            link(dve.reciprocal(rden[:, :, :], o4[:, :, :, D]))
                            g = n % G
                            dve.tensor_tensor(
                                o_nat[:, :, HG * D * g:HG * D * (g + 1)].rearrange("p q (h d) -> p q h d", d=D),
                                o4[:, :, :, 0:D],
                                rden[:, :, :].rearrange("p q (h o) -> p q h o", o=1).to_broadcast([P, QT, HG, D]),
                                ALU.mult).then_inc(misc_free, 1)
                        elif what in ("proj0", "proj1"):
                            wait_turn()
                            j = int(what[-1])
                            rows = x_sb[:, bass.ds((i + n) * QT + 2 * j, 2), :].rearrange("p o c -> p (o c)")
                            dve.wait_ge(xb_done, 1)
                            dve.scalar_tensor_tensor(out=rows, in0=MISC, scalar=tanh_g[:, 0:1], in1=rows,
                                                     op0=ALU.mult, op1=ALU.add).then_inc(misc_free, 1)
                        elif what == "norm2":
                            dve.wait_ge(misc_free, turn.at())
                            rt.step()
                            dve.wait_ge(xd_free, rt.at())
                            layer_norm(xd, i + n, x1_done)
                        elif what == "router":
                            wait_turn()
                            lg = MISC[:, 0:QT * E].rearrange("p (q e) -> p q e", e=E)
                            link(dve.tensor_reduce(lmax[:, :], lg, AX_X, ALU.max))
                            dve.tensor_tensor(lshift[:, :, :], lg, per_row(lmax[:, :], E, [P, QT, E]),
                                              ALU.subtract).then_inc(misc_free, 1)
                        elif what == "top2":
                            dve.wait_ge(lexp_done, rt.at())
                            link(dve.tensor_reduce(lsum[:, :], lexp[:, :, :], AX_X, ALU.add))
                            link(dve.reciprocal(lsum[:, :], lsum[:, :]))
                            link(dve.tensor_tensor(score[:, :, :], lexp[:, :, :],
                                                   per_row(lsum[:, :], E, [P, QT, E]), ALU.mult))
                            hold()
                            for t in range(QT):
                                ins = dve.max(top[:, t, :], score[:, t, :])
                            link(ins)
                            hold()
                            for t in range(QT):
                                ins = dve.max_index(top_e[:, t, :], top[:, t, :], score[:, t, :])
                            link(ins)
                            link(dve.tensor_copy(top_ef[:, :, :], top_e[:, :, 0:TOPK]))
                            for k in range(TOPK):
                                ins = dve.tensor_tensor(
                                    hot[:, :, k * E:(k + 1) * E],
                                    iota_e[:, :].rearrange("p (o e) -> p o e", o=1).to_broadcast([P, QT, E]),
                                    per_row(top_ef[:, :, k], E, [P, QT, E]), ALU.is_equal)
                            ins.then_inc(hot_done, 1)
                            dve.tensor_scalar(xd[:, :, C:C + TOPK], top[:, :, 0:TOPK], tanh_g[:, 1:2], None, ALU.mult)
                            dve.tensor_copy(xd[:, :, C + TOPK:ROW].rearrange("p q o -> p (q o)"),
                                            token_no[:, bass.ds((i + n) * QT, QT)]).then_inc(xd_done, 1)
                        elif what == "ranks":
                            wait_turn()
                            rk = MISC[:, 0:QT * TOPK * E].rearrange("p (q n) -> p q n", n=TOPK * E)
                            base = slot_base[:, :, :].rearrange("p (o k) e -> p o (k e)", o=1) \
                                .to_broadcast([P, QT, TOPK * E])
                            dve.tensor_tensor(pos[:, :, :], rk, base, ALU.add)
                            dve.tensor_scalar(over[:, :, :], rk, float(CAP), float(DROPPED), ALU.is_ge, ALU.mult) \
                                .then_inc(misc_free, 1)
                            link(dve.tensor_reduce(hot_sum[:, :], hot[:, :, :].rearrange("p q n -> p n q"),
                                                   AX_X, ALU.add))
                            dve.wait_ge(misc_free, turn.at())
                            dve.tensor_tensor(carry[:, :], carry[:, :], hot_sum[:, :], ALU.add)
                            link(dve.tensor_tensor(pos[:, :, :], pos[:, :, :], over[:, :, :], ALU.add))
                            link(dve.tensor_tensor(pos[:, :, :], pos[:, :, :], hot[:, :, :], ALU.mult))
                            link(dve.tensor_reduce(slot_f[:, :, :], pos[:, :, :].rearrange("p q (k e) -> p q k e", e=E),
                                                   AX_X, ALU.add))
                            dve.tensor_copy(slot_u[:, :, :], slot_f[:, :, :]).then_inc(slot_done, 1)
                        elif what in SHARED:
                            turn.step()

            for u in range(LEAD):
                row_max(u)
            turn.step()
            run_steps(dve, steps, [(unit, PERIOD), (turn, TURNS), (rt, 1),
                                   (link_n, G + NORM_LINKS + 1 + 8 + 4)])

            def cut_weights(k, step):
                if step in (0, 3):
                    raw, hi = (w1_raw, w1_p) if step == 0 else (w2_raw, w2_p)
                    return dve.tensor_copy(hi[k][0][:, :, :], raw[k][:, :, :])
                raw, part = (w1_raw, w1_p) if step < 3 else (w2_raw, w2_p)
                flat = [x[:, :, :].rearrange("p a b -> p (a b)") for x in (part[k][1], raw[k], part[k][0])]
                half = slice((step % 3 - 1) * F, (step % 3) * F)
                return dve.tensor_tensor(flat[0][:, half], flat[1][:, half], flat[2][:, half], ALU.subtract)

            def cut_rows(n, k):
                dve.wait_ge(rows_added, n + 1)
                dve.tensor_copy(tok_u[k][:, :], xe[k][:, :, ROW - 1]).then_inc(tok_done, 1)
                for c in range(2):
                    dve.wait_ge(xeT_ready, n * 2 + (c + 1))
                    link(dve.tensor_copy(xeT[0][:, c, :], bank(c)))
                    dve.tensor_tensor(xeT[1][:, c, :], bank(c), xeT[0][:, c, :], ALU.subtract).then_inc(xeT_done, 1)

            def results(n, k):
                for s in range(SPE):
                    dve.wait_ge(y_ready, n * SPE + (s + 1))
                    w = C + s * P // CAP
                    dve.tensor_scalar(y_sb[k][:, s, :], bank(6 + s % 2)[:, 0:C], xe[k][:, s, w:w + 1], None,
                                      ALU.mult).then_inc(y_done, 1)

            def hidden(n, k, more):
                if more:
                    cut_in(n + 1, 1 - k)
                for f in range(FT):
                    dve.wait_ge(hhi_done, n * FT + (f + 1))
                    dve.tensor_tensor(hid_p[1][:, f, :], hid[:, f % 4, :], hid_p[0][:, f, :], ALU.subtract) \
                        .then_inc(hid_done, 1)
                    if more and f < 6:
                        ins = cut_weights(1 - k, f)
                        if f == 5:
                            ins.then_inc(w_cut, 1)
                        else:
                            link(ins)

            def cut_in(n, k):
                dve.wait_ge(w_raw_in[k], raw_n(n, k))

            def raw_n(n, k):
                return (n - k) * 16 + 32

            dve.wait_ge(xe_in[0], 16)
            cut_in(0, 0)
            for step in range(5):
                link(cut_weights(0, step))
            cut_weights(0, 5).then_inc(w_cut, 1)
            cut_rows(0, 0)
            hidden(0, 0, True)

            def expert(n, k, more=True):
                dve.wait_ge(xe_in[k], (n - k) * 8 + 16)
                cut_rows(n, k)
                results(n - 1, 1 - k)
                hidden(n, k, more)

            with dve.Fori(0, (E - 2) // 2) as j:
                link_n.begin(j, 2 * (2 + 5))
                expert(j * 2 + 1, 1)
                expert(j * 2 + 2, 0)
                link_n.end((E - 2) // 2)
            expert(E - 1, 1, more=False)
            results(E - 1, 1)

        @block.tensor
        def _(pe):
            pe.wait_ge(w_in, 16)
            pe.wait_ge(consts_done, 1)
            with pe.Fori(0, B) as b:
                pe.wait_ge(xn_done, b + 1)
                for k in range(2):
                    pe.wait_ge(xnT_done, b * 2 + (k + 1))
                    for t in range(QT):
                        mm = pe.transpose(bank(k)[:, t * P:(t + 1) * P], xn[:, t, k * P:(k + 1) * P], ident[:, :])
                    mm.then_inc(xnT_ready, 1)
                pe.wait_ge(xnT_done, b * 2 + 4)
                for m in range(4):
                    pe.wait_ge(qkv_out, b * 6 + (m + 1))
                    for k in range(2):
                        mm = pe.matmul(bank(2 + m), w_qkv[:, k, m * P:(m + 1) * P], xnT[:, k, :],
                                       start=(k == 0), stop=(k == 1))
                    mm.then_inc(qkv_ready, 1)
                for j in range(2):
                    pe.wait_ge(qkv_out, b * 6 + (5 + j))
                    for t in range(2):
                        for k in range(2):
                            mm = pe.matmul(bank(6 + j)[:, t * C:(t + 1) * C],
                                           xnT[:, k, (2 * j + t) * P:(2 * j + t + 1) * P], w_qkv[:, k, 2 * C:3 * C],
                                           start=(k == 0), stop=(k == 1))
                    mm.then_inc(qkv_ready, 1)
            pe.wait_ge(qkv_out, 6 * (B + 1))

            unit, st, pv, turn, group, rt = (Tally() for _ in range(6))

            def max_scores(u, i=0):
                g, j = u // SLOTS_PER_GROUP, u % SLOTS_PER_GROUP
                head, qt = g % G * HG + j // QT, j % QT
                if j == 0:
                    pe.wait_ge(qk_in[g % G], (i + (g // G + 1)) * (2 * 16 * len(PAIRS)))
                if u >= 2:
                    pe.wait_ge(max_done, unit.at(-1))
                for half in range(2):
                    mm = pe.matmul(bank(2 * (u % 2) + half), q6[0:KROWS, head, qt * P:(qt + 1) * P],
                                   k6[0:KROWS, head, half * 512:(half + 1) * 512], start=True, stop=True)
                mm.then_inc(s_ready, 1)
                unit.step()

            def take_turn(u=None):
                if u is None:
                    pe.wait_ge(misc_free, turn.at())
                turn.step()

            def turn_max(g, first=False):
                pe.wait_ge(max_done, group_units(g))
                take_turn(0 if first else None)
                pe.transpose(MISC[0:SLOTS_PER_GROUP, 0:P], mx[:, g % 2, :], ident[:, :]).then_inc(misc_ready, 1)

            tm = Tally()

            def group_units(g):
                tm.step()
                return tm.at() * SLOTS_PER_GROUP

            def steps(c0, c1, i=0):
                for c in range(c0, c1):
                    s = c % SLOTS_PER_GROUP
                    for what, n in steps_at(c):
                        if what == "max":
                            max_scores(n, i)
                        elif what == "scores":
                            g, kt, pair = c // SLOTS_PER_GROUP, s // 2, s % 2
                            if s == 0:
                                pe.wait_ge(shift_in[g % G], (i + (g // G + 1)) * (16 * NPART))
                            for j in range(2):
                                head = g % G * HG + 2 * pair + j
                                if c >= 1:
                                    pe.wait_ge(exp_done, st.at(-1))
                                pe.matmul(bank(4 + j), k6[0:AROWS, head, kt * P:(kt + 1) * P], q6[0:AROWS, head, :],
                                          start=True, stop=True).then_inc(st_ready, 1)
                                st.step()
                        elif what == "values":
                            g = (c - 2) // SLOTS_PER_GROUP
                            if n == 0:
                                group.step()
                                pe.wait_ge(v_set, group.at())
                                if c >= SLOTS_PER_GROUP:
                                    pe.wait_ge(o_copied, group.at(-1))
                            pv.step()
                            pe.wait_ge(exp_done, pv.at() * HG)
                            for j in range(HG):
                                mm = pe.matmul(bank(6)[j * 2 * D:(j + 1) * 2 * D, :],
                                               v_ones[:, n, g % G * HG + j, :], pexp[n % NP][:, j, :],
                                               start=(n == 0), stop=(n == KT - 1))
                            mm.then_inc(pv_done, 1)
                        elif what == "turn_out":
                            pe.wait_ge(o_copied, group.at(to_out(c)))
                            take_turn()
                            for q in range(QT):
                                mm = pe.transpose(MISC[:, q * P:(q + 1) * P], o_t[:, q * P:(q + 1) * P], ident[:, :])
                            mm.then_inc(misc_ready, 1)
                        elif what == "turn_max":
                            turn_max(n)
                        elif what in ("attn_t0", "attn_t1", "x1_t0", "x1_t1"):
                            k = int(what[-1])
                            take_turn()
                            if what == "attn_t0":
                                rt.step()
                            if what == "x1_t0":
                                pe.wait_ge(x1_done, rt.at())
                            src = o_nat if what[0] == "a" else xd
                            for q in range(QT):
                                mm = pe.transpose(MISC[:, q * P:(q + 1) * P], src[:, q, k * P:(k + 1) * P], ident[:, :])
                            mm.then_inc(misc_ready, 1)
                        elif what in ("proj0", "proj1"):
                            j = int(what[-1])
                            take_turn()
                            pe.wait_ge(consts_in, 4 * 16)
                            for t in range(2):
                                for k in range(2):
                                    mm = pe.matmul(MISC[:, t * C:(t + 1) * C],
                                                   o_natT[:, k, (2 * j + t) * P:(2 * j + t + 1) * P], w_p[:, k, :],
                                                   start=(k == 0), stop=(k == 1))
                            mm.then_inc(misc_ready, 1)
                        elif what == "router":
                            take_turn()
                            for t in range(QT):
                                for k in range(2):
                                    mm = pe.matmul(MISC[:, t * E:(t + 1) * E], x1T[:, k, t * P:(t + 1) * P],
                                                   w_r[:, k, :], start=(k == 0), stop=(k == 1))
                            mm.then_inc(misc_ready, 1)
                        elif what == "ranks":
                            take_turn()
                            pe.wait_ge(hot_done, rt.at())
                            n16 = TOPK * E
                            for t in range(QT):
                                dst = MISC[:, t * n16:(t + 1) * n16]
                                pe.matmul(dst, below[:, :], hot[:, t, :], start=True, stop=False)
                                for before in range(t):
                                    pe.matmul(dst, ones[:, :], hot[:, before, :], start=False, stop=False)
                                mm = pe.matmul(dst, ones[:, :], carry[:, :], start=False, stop=True)
                            mm.then_inc(misc_ready, 1)

            def to_out(c):
                return -1 if c < STEPS else 0

            pe.wait_ge(k_ones, 16)
            for u in range(LEAD):
                max_scores(u)
                if u == SLOTS_PER_GROUP + 2:
                    turn_max(0, first=True)
            run_steps(pe, steps, [(unit, PERIOD), (st, 2 * PERIOD), (pv, G * KT), (turn, TURNS), (group, G),
                                  (rt, 1), (tm, G)])

            def rows(n, k):
                pe.wait_ge(xe_in[k], (n - k) * 8 + 16)
                for c in range(2):
                    for s in range(SPE):
                        mm = pe.transpose(bank(c)[:, s * P:(s + 1) * P], xe[k][:, s, c * P:(c + 1) * P], ident[:, :])
                    mm.then_inc(xeT_ready, 1)

            PASSES = [(0, 0), (0, 1), (1, 0)]

            def hidden(n, k):
                pe.wait_ge(w_cut, n + 1)
                pe.wait_ge(xeT_done, (n + 1) * 2)
                for f in range(FT):
                    pe.wait_ge(h_out, n * FT + (f + 1))
                    terms = [(c, a, b) for c in range(2) for a, b in PASSES]
                    for c, a, b in terms:
                        mm = pe.matmul(bank(2 + f % 4), w1_p[k][a][:, c, f * P:(f + 1) * P], xeT[b][:, c, :],
                                       start=(c, a, b) == terms[0], stop=(c, a, b) == terms[-1])
                    mm.then_inc(h_ready, 1)

            def results(n, k):
                pe.wait_ge(hid_done, (n + 1) * FT + 4)
                for s in range(SPE):
                    pe.wait_ge(y_done, n * SPE + (s + 1))
                    terms = [(f, a, b) for f in range(FT) for a, b in PASSES]
                    for f, a, b in terms:
                        mm = pe.matmul(bank(6 + s % 2)[:, 0:C], hid_p[a][:, f, s * P:(s + 1) * P], w2_p[k][b][:, f, :],
                                       start=(f, a, b) == terms[0], stop=(f, a, b) == terms[-1])
                    mm.then_inc(y_ready, 1)

            rows(0, 0)
            hidden(0, 0)
            with pe.Fori(0, (E - 2) // 2) as j:
                rows(j * 2 + 1, 1)
                results(j * 2, 0)
                hidden(j * 2 + 1, 1)
                rows(j * 2 + 2, 0)
                results(j * 2 + 1, 1)
                hidden(j * 2 + 2, 0)
            rows(E - 1, 1)
            results(E - 2, 0)
            hidden(E - 1, 1)
            results(E - 1, 1)


_OUT = ((B, T, C), "float32")


def kernel(**inputs):
    import concourse.bacc as _bacc
    import numpy as _np
    from concourse.bass_utils import run_bass_kernel_spmd as _run

    a = {k: _np.asarray(v) for k, v in inputs.items()}
    ctx = a["ctx_2048"]
    arrays = {
        "x": a["x"].reshape(NTOK, C),
        "ctx_kT": ctx[:, :, 0:C].transpose(0, 2, 1),
        "ctx_v": ctx[:, :, C:2 * C],
        "g_xattn": a["g_xattn"].reshape(1, 1),
        "g_ffn": a["g_ffn"].reshape(1, 1),
        "w_qkvT": a["L0_xattn_w_qkv"].T,
        "w_projT": a["L0_xattn_w_proj"].T,
        "b_proj": a["L0_xattn_b_proj"].reshape(1, C),
        "router_w": a["L0_ffn_router_w"],
        "w1": a["L0_ffn_w1"],
        "w2": a["L0_ffn_w2"],
        "bias": a["L0_ffn_bias"].reshape(1, C),
    }
    arrays = {k: _np.ascontiguousarray(v) for k, v in arrays.items()}
    nc = _bacc.Bacc("TRN2", target_bir_lowering=False, num_devices=1)
    args = [nc.dram_tensor(k, v.shape, mybir.dt.from_np(v.dtype), kind="ExternalInput").ap()
            for k, v in arrays.items()]
    args.append(nc.dram_tensor("out", (NTOK, C), F32, kind="ExternalOutput").ap())
    build(nc, *args)
    r = _run(nc, [arrays], core_ids=[0])
    return r.results[0]["out"].reshape(_OUT[0])
```

```python
from contextlib import ExitStack

import concourse.bass as bass
from concourse import mybir

ALU = mybir.AluOpType
ACT = mybir.ActivationFunctionType
F32 = mybir.dt.float32
F32R = mybir.dt.float32r
BF16 = mybir.dt.bfloat16
U32 = mybir.dt.uint32
I32 = mybir.dt.int32
AX_X = mybir.AxisListType.X

P = 128
B, T, C = 4, 512, 256
H, D = 16, 16
TC = 512
NKEY = TC + T
KT = NKEY // P
QT = T // P
G, HG = 4, 4
NGROUP = B * G
E, F, TOPK = 8, 1024, 2
NTOK = B * T
CAP = NTOK // E
SLOTS = TOPK * CAP
NSLOT = E * SLOTS
ROW = C + TOPK + 1
NPART = 3
PAIRS = [(0, 0), (0, 1), (0, 2), (1, 0), (1, 1), (2, 0)]
KROWS = len(PAIRS) * D
AROWS = KROWS + NPART
EPS = 1e-5
ROOT_SEED = 1597463007.0
NEWTON = 3
NORM_LINKS = 6 + 3 * NEWTON
NOBODY = 1 << 20
DROPPED = 1 << 16

SLOTS_PER_GROUP = 16
STEPS = NGROUP * SLOTS_PER_GROUP
PERIOD = G * SLOTS_PER_GROUP
LEAD = 24
TURN = PERIOD - LEAD
UNITS_AFTER = {B - 2: (2, 2, 2, 2, 2), B - 1: (2, 2, 2, 4, 4)}
NP = 4


def steps_at(c):
    s, p, g = c % SLOTS_PER_GROUP, c % PERIOD, c // SLOTS_PER_GROUP
    behind = 1 <= g <= NGROUP
    if behind and s == 1:
        yield "copy_out", g - 1
    if c < STEPS:
        yield "scores", c
    if 2 <= c <= STEPS and s % 2 == 0:
        yield "values", (s // 2 - 1) % KT
    if s % 2 and c + LEAD < STEPS:
        yield "max", c + LEAD - 1
        yield "max", c + LEAD
    if behind and s == 1 and g + 3 < NGROUP:
        yield "load", g + 3
    if s == 2 and g >= 3 and g + 1 < NGROUP:
        yield "set_v", g + 1
    if behind and s == 5:
        yield "turn_out", g - 1
    if s == 10 and g + 1 < NGROUP:
        yield "turn_max", g + 1
    for name in ROUTE_AT.get(p, []) if c >= PERIOD else []:
        yield name, c // PERIOD - 1


ROUTE_AT = {7: ["attn_t0"], 8: ["attn_t1"], 12: ["proj0"], 14: ["proj1"], 15: ["norm2"],
            23: ["x1_t0"], 24: ["x1_t1"], 29: ["router"], 31: ["top2"], 34: ["ranks"], 37: ["scatter"]}
SHARED = ("turn_out", "turn_max", "attn_t0", "attn_t1", "proj0", "proj1", "x1_t0", "x1_t1", "router",
          "ranks")
TURNS = 2 * G + 8


class Tally:

    def __init__(self):
        self.n, self.reg, self.per = 0, None, 0

    def step(self, m=1):
        self.n += m

    def at(self, d=0):
        return self.n + d if self.reg is None else self.reg * self.per + (self.n + d)

    def begin(self, reg, per):
        self.reg, self.per, self.n0 = reg, per, self.n

    def end(self, turns):
        assert self.n - self.n0 == self.per, (self.n - self.n0, self.per)
        self.n, self.reg = self.n0 + self.per * turns, None


def build(nc, x_in, ctx_kT, ctx_v, g_x, g_f, w_qkvT, w_projT, b_proj, router_w, w1, w2, bias, out):
    stack = ExitStack()
    phase1 = ExitStack()
    phase2 = ExitStack()

    def sb(name, shape, dt, where=stack):
        return where.enter_context(nc.sbuf_tensor(name, shape, dt))

    def sem(name):
        return stack.enter_context(nc.semaphore(name))

    with stack:
        ident = sb("ident", [P, P], F32)
        below = sb("below", [P, P], BF16)
        ones = sb("ones", [P, P], BF16)
        iota_e = sb("iota_e", [P, E], F32)
        slot_base = sb("slot_base", [P, TOPK, E], F32)
        token_no = sb("token_no", [P, B * QT], F32)
        gates = sb("gates", [P, 2], F32)
        tanh_g = sb("tanh_g", [P, 2], F32)
        b_row = sb("b_row", [P, C], F32)
        bias_row = sb("bias_row", [P, C], F32)
        x_sb = sb("x_sb", [P, B * QT, C], F32)
        w1_raw = [sb("w1_raw0", [P, 2, F], F32)]
        w2_raw = [sb("w2_raw0", [P, F // P, C], F32)]
        stats = sb("stats", [P, QT, 6], F32)
        meanvar = sb("meanvar", [P, QT, 2], F32)
        rstd = sb("rstd", [P, QT], F32)
        var = sb("var", [P, QT], F32)
        held_p = sb("held_p", [P, 10], F32)
        held = sb("held", [P, 2], F32)
        root_t = sb("root_t", [P, QT], F32)

        k6 = sb("k6", [P, H, NKEY], BF16, phase1)
        q6 = sb("q6", [P, H, T], BF16, phase1)
        v_stash = sb("v_stash", [P, 2, B, QT, C], F32, phase1)
        v_ones = sb("v_ones", [P, KT, H, 2 * D], F32, phase1)
        o_t = sb("o_t", [P, T], F32, phase1)
        o_nat = sb("o_nat", [P, QT, C], F32, phase1)
        o_natT = sb("o_natT", [P, 2, T], F32, phase1)
        w_p = sb("w_p", [P, 2, C], F32, phase1)
        w_r = sb("w_r", [P, 2, E], F32, phase1)
        xd = sb("xd", [P, QT, ROW], F32, phase1)
        x1T = sb("x1T", [P, 2, T], F32, phase1)
        rden = sb("rden", [P, QT, HG], F32, phase1)
        mx = sb("mx", [P, 2, SLOTS_PER_GROUP], F32, phase1)
        neg_m = sb("neg_m", [SLOTS_PER_GROUP, P], F32, phase1)
        neg_parts = sb("neg_parts", [SLOTS_PER_GROUP, NPART, P], BF16, phase1)
        lmax = sb("lmax", [P, QT], F32, phase1)
        lshift = sb("lshift", [P, QT, E], F32, phase1)
        lexp = sb("lexp", [P, QT, E], F32, phase1)
        lsum = sb("lsum", [P, QT], F32, phase1)
        score = sb("score", [P, QT, E], F32, phase1)
        top = sb("top", [P, QT, 8], F32, phase1)
        top_e = sb("top_e", [P, QT, 8], U32, phase1)
        top_ef = sb("top_ef", [P, QT, TOPK], F32, phase1)
        hot = sb("hot", [P, QT, TOPK * E], BF16, phase1)
        hot_sum = sb("hot_sum", [P, TOPK * E], F32, phase1)
        carry = sb("carry", [P, TOPK * E], BF16, phase1)
        pos = sb("pos", [P, QT, TOPK * E], F32, phase1)
        over = sb("over", [P, QT, TOPK * E], F32, phase1)
        slot_f = sb("slot_f", [P, QT, TOPK], F32, phase1)
        slot_u = sb("slot_u", [P, QT, TOPK], U32, phase1)
        parts = sb("parts", [P, NPART, 4, T], BF16, phase1)
        c_parts = sb("c_parts", [P, NPART, 2, T], BF16, phase1)
        empty = sb("empty", [P, ROW], F32, phase1)
        with ExitStack() as early:
            xn = sb("xn", [P, QT, C], F32, early)
            xnT = sb("xnT", [P, 2, T], F32, early)
            w_qkv = sb("w_qkv", [P, 2, 3 * C], F32, early)
            qk = sb("qk", [P, 4, T], F32, early)
            ctxk = sb("ctxk", [P, 2, T], F32, early)
        pexp = [sb(f"pexp{i}", [P, HG, T], F32, phase1) for i in range(NP)]
        phase1.close()

        w1_p = [[sb(f"w1_{h}0", [P, 2, F], F32R, phase2) for h in ("hi", "lo")]]
        w2_p = [[sb(f"w2_{h}0", [P, F // P, C], F32R, phase2) for h in ("hi", "lo")]]
        w1_raw.append(sb("w1_raw1", [P, 2, F], F32, phase2))
        w2_raw.append(sb("w2_raw1", [P, F // P, C], F32, phase2))
        xe = [sb(f"xe{i}", [P, SLOTS // P, ROW], F32, phase2) for i in range(2)]
        tok_u = [sb(f"tok_u{i}", [P, SLOTS // P], U32, phase2) for i in range(2)]
        xeT = [sb(f"xeT_{h}", [P, 2, SLOTS], F32R, phase2) for h in ("hi", "lo")]
        w1_p.append([sb(f"w1_{h}1", [P, 2, F], F32R, phase2) for h in ("hi", "lo")])
        w2_p.append([sb(f"w2_{h}1", [P, F // P, C], F32R, phase2) for h in ("hi", "lo")])
        hid = sb("hid", [P, 4, SLOTS], F32, phase2)
        hid_p = [sb(f"hid_{h}", [P, F // P, SLOTS], F32R, phase2) for h in ("hi", "lo")]
        y_sb = [sb(f"y_sb{i}", [P, SLOTS // P, C], F32, phase2) for i in range(2)]
        phase2.close()

        ps = stack.enter_context(nc.psum_tensor("ps", [P, 8, 512], F32))

        q_dram = nc.dram_tensor("q_parts", (B, NPART, C, T), BF16, kind="Internal").ap()
        k_dram = nc.dram_tensor("k_parts", (B, NPART, C, NKEY), BF16, kind="Internal").ap()
        slot_dram = nc.dram_tensor("slot_rows", (NSLOT, ROW), F32, kind="Internal").ap()

        chain_v, chain_p = sem("chain_v"), sem("chain_p")
        x0_in = sem("x0_loaded")
        consts_in, x_in_s, w_in, vctx_in, ctxk_in = (sem(n) for n in (
            "consts_in", "x_loaded", "w_loaded", "vctx_loaded", "ctxk_loaded"))
        gate_in, gates_done = sem("gates_loaded"), sem("gates_done")
        consts_done, empty_done, empty_out = sem("consts_done"), sem("empty_done"), sem("empty_out")
        xn_done, xnT_ready, xnT_done = sem("xn_done"), sem("xnT_ready"), sem("xnT_done")
        qkv_ready, qkv_out = sem("qkv_ready"), sem("qkv_out")
        parts_done, cparts_done = sem("parts_done"), sem("cparts_done")
        parts_out, cparts_out = [sem("q_parts_stored"), sem("k_parts_stored")], sem("cparts_stored")
        xb_done = sem("xb_done")
        one_row, k_ones = sem("one_row"), sem("k_ones")
        qk_in = [sem(f"qk_loaded{g}") for g in range(G)]
        shift_in = [sem(f"shift_in{g}") for g in range(G)]
        s_ready, max_done = sem("max_scores_ready"), sem("max_done")
        st_ready, exp_done = sem("scores_ready"), sem("exp_done")
        pv_done, o_copied = sem("pv_done"), sem("o_copied")
        v_set = sem("v_set")
        misc_ready, misc_free = sem("misc_ready"), sem("misc_free")
        shift_done = sem("shift_parts_done")
        x1_done, xd_done = sem("x1_done"), sem("xd_done")
        lexp_done, hot_done, slot_done = sem("lexp_done"), sem("hot_done"), sem("slot_done")
        res_done, res_out, scattered = sem("residual_done"), sem("residual_stored"), sem("scattered")
        w_raw_in = [sem(f"w_raw_in{i}") for i in range(2)]
        xe_in = [sem(f"xe_in{i}") for i in range(2)]
        xeT_ready, xeT_done = sem("xeT_ready"), sem("xeT_done")
        w_hi, w1_lo, w2_lo = sem("w_hi"), sem("w1_lo"), sem("w2_lo")
        h_ready, h_out, hid_done = sem("h_ready"), sem("h_out"), sem("hid_done")
        hhi_done, y_ready, y_done = sem("hhi_done"), sem("y_ready"), sem("y_done")
        tok_done, added, rows_added = sem("tok_done"), sem("added"), sem("rows_added")
        xd_free = sem("xd_free")

        def bank(i, n=1):
            return ps[:, i, :] if n == 1 else ps[:, i:i + n, :]

        def pieces(x):
            flat = x[:, :, :].rearrange("p a b -> p (a b)")
            return [flat[:, 0:F], flat[:, F:2 * F]]

        MISC = bank(7)
        SPE = SLOTS // P
        FT = F // P

        def run_steps(eng, steps, tallies, turn=TURN):
            steps(0, turn)
            with eng.Fori(0, B - 1) as i:
                for t, per in tallies:
                    t.begin(i, per)
                steps(turn, turn + PERIOD, i)
                for t, per in tallies:
                    t.end(B - 1)
            steps(turn + PERIOD * (B - 1), STEPS + PERIOD)

        block = stack.enter_context(nc.Block())

        @block.sync
        def _(sp):
            st, shifts = Tally(), Tally()

            def load_ctxk(b):
                sp.wait_ge(cparts_done, b + 1)
                sp.dma_start(ctxk[:, :, :], ctx_kT[b].rearrange("(m p) t -> p m t", p=P)).then_inc(ctxk_in, 16)

            def store_parts(b):
                sp.wait_ge(cparts_done, b + 2)
                for i in range(NPART):
                    sp.dma_start(k_dram[b, i, :, 0:TC].rearrange("(m p) t -> p m t", p=P),
                                 c_parts[:, i, :, :]).then_inc(cparts_out, 16)
                if b + 1 < B:
                    load_ctxk(b + 1)
                sp.wait_ge(parts_done, 2 * b + 3)
                for i in range(NPART):
                    sp.dma_start(q_dram[b, i].rearrange("(m p) t -> p m t", p=P),
                                 parts[:, i, 0:2, :]).then_inc(parts_out[0], 16)
                sp.wait_ge(parts_done, 2 * b + 4)
                for i in range(NPART):
                    sp.dma_start(k_dram[b, i, :, TC:NKEY].rearrange("(m p) t -> p m t", p=P),
                                 parts[:, i, 2:4, :]).then_inc(parts_out[1], 16)

            def wait_stored(b):
                for half in range(2):
                    sp.wait_ge(parts_out[half], 3 * 16 * (b + 2))
                sp.wait_ge(cparts_out, 3 * 16 * (b + 2))

            def fill_slots(half):
                n = NSLOT // P // 2
                sp.wait_ge(empty_done, 1)
                sp.dma_start(slot_dram.rearrange("(n p) c -> p n c", p=P)[:, half * n:(half + 1) * n, :],
                             empty[:, :].rearrange("p (o c) -> p o c", o=1).to_broadcast([P, n, ROW])) \
                    .then_inc(empty_out, 16)

            def shift_rows(g):
                sp.wait_ge(shift_done, shifts.at())
                for i in range(NPART):
                    sp.dma_start(q6[KROWS + i:KROWS + i + 1, HG * g:HG * (g + 1), :]
                                 .rearrange("o h (q t) -> o (h q) t", t=P),
                                 neg_parts[:, i, :]).then_inc(shift_in[g], 16)

            def load_weights(e, k):
                sp.dma_start(w1_raw[k][:, :, :], w1[bass.ds(e, 1)].rearrange("a (k p) f -> p (a k) f", p=P)) \
                    .then_inc(w_raw_in[k], 16)
                sp.dma_start(w2_raw[k][:, :, :], w2[bass.ds(e, 1)].rearrange("a (k p) c -> p (a k) c", p=P)) \
                    .then_inc(w_raw_in[k], 16)

            def load_rows(e, k):
                sp.dma_start(xe[k][:, :, :], slot_dram[bass.ds(e * SLOTS, SLOTS), :]
                             .rearrange("(s p) c -> p s c", p=P)).then_inc(xe_in[k], 16)

            def load_group(b, g):
                for r, (pq, pk) in enumerate(PAIRS):
                    sp.dma_start(q6[r * D:(r + 1) * D, HG * g:HG * (g + 1), :],
                                 q_dram[bass.ds(b, 1), pq, HG * D * g:HG * D * (g + 1), :]
                                 .rearrange("a (h d) t -> d (a h) t", d=D)).then_inc(qk_in[g], 16)
                    sp.dma_start(k6[r * D:(r + 1) * D, HG * g:HG * (g + 1), :],
                                 k_dram[bass.ds(b, 1), pk, HG * D * g:HG * D * (g + 1), :]
                                 .rearrange("a (h d) t -> d (a h) t", d=D)).then_inc(qk_in[g], 16)

            for half in range(2):
                sp.sem_inc(parts_out[half], 3 * 16)
            sp.dma_start(x_sb[:, 0:QT, :], x_in[0:T, :].rearrange("(t p) c -> p t c", p=P)).then_inc(x0_in, 16)
            sp.dma_start(w_qkv[:, :, :], w_qkvT.rearrange("(k p) n -> p k n", p=P)).then_inc(w_in, 16)
            load_ctxk(0)
            sp.dma_start(gates[:, 0:1], g_x.broadcast_to([P, 1])).then_inc(gate_in, 16)
            sp.dma_start(gates[:, 1:2], g_f.broadcast_to([P, 1])).then_inc(gate_in, 16)
            sp.dma_start(x_sb[:, QT:, :], x_in[T:, :].rearrange("(t p) c -> p t c", p=P)).then_inc(x_in_s, 16)
            sp.wait_ge(one_row, 1)
            sp.dma_start(k6[KROWS:AROWS, 1:H, :], k6[KROWS:AROWS, 0:1, :].to_broadcast([NPART, H - 1, NKEY])) \
                .then_inc(k_ones, 16)
            sp.dma_start(b_row[:, :], b_proj.broadcast_to([P, C])).then_inc(consts_in, 16)
            sp.dma_start(bias_row[:, :], bias.broadcast_to([P, C])).then_inc(consts_in, 16)
            sp.dma_start(w_p[:, :, :], w_projT.rearrange("(k p) n -> p k n", p=P)).then_inc(consts_in, 16)
            sp.dma_start(w_r[:, :, :], router_w.rearrange("(k p) n -> p k n", p=P)).then_inc(consts_in, 16)
            sp.dma_start(v_stash[:, 0, :, :, :].rearrange("p b t c -> p (b t) c"),
                         ctx_v.rearrange("b (t p) c -> p (b t) c", p=P)).then_inc(vctx_in, 16)
            store_parts(0)
            wait_stored(0)
            load_group(0, 0)
            fill_slots(0)
            store_parts(1)
            load_group(0, 1)
            fill_slots(1)
            load_weights(0, 0)
            store_parts(2)
            load_group(0, 2)
            load_group(0, 3)
            shifts.step()
            shift_rows(0)
            store_parts(3)
            wait_stored(B - 1)

            def steps(c0, c1, i=0):
                for c in range(c0, c1):
                    for what, n in steps_at(c):
                        if what == "scores":
                            st.step(2)
                        elif what == "load":
                            sp.wait_ge(st_ready, st.at(-4))
                            load_group(i + n // G, n % G)
                        elif what == "turn_max":
                            shifts.step()
                            shift_rows(n % G)

            run_steps(sp, steps, [(st, 2 * PERIOD), (shifts, G)], turn=2)

            sp.wait_ge(st_ready, 2 * STEPS)
            load_weights(1, 1)
            sp.wait_ge(pv_done, NGROUP * KT)
            sp.wait_ge(scattered, B * QT * TOPK * 16)
            load_rows(0, 0)
            load_rows(1, 1)

            def reload(n, k):
                sp.wait_ge(w1_lo, n * 2 + 2)
                sp.wait_ge(w2_lo, n * 2 + 2)
                load_weights(n + 2, k)
                sp.wait_ge(y_done, (n + 1) * SPE + 2)
                load_rows(n + 2, k)

            with sp.Fori(0, (E - 2) // 2) as j:
                reload(j * 2, 0)
                reload(j * 2 + 1, 1)
            sp.wait_ge(added, E * SPE * 16)

        @block.gpsimd
        def _(pool):
            link_n = Tally()

            def link(ins):
                ins.then_inc(chain_p, 1)
                link_n.step()
                pool.wait_ge(chain_p, link_n.at())

            def touch(k):
                return pool.tensor_tensor(held_p[:, k:k + 1], held_p[:, 9:10], held_p[:, 9:10], ALU.mult)

            def hold(k):
                touch(k).then_inc(chain_p, 1)
                link_n.step()

            def copy(dst, src):
                names = {2: "p (a) -> p a", 3: "p (a b) -> p a b", 4: "p (a b c) -> p a b c"}[len(src.shape)]
                units = {k: 1 for k in "abc"[:len(src.shape) - 2]}
                one = held_p[0:src.shape[0], 9:10].rearrange(names, **units)
                return pool.tensor_tensor(dst, src, one.to_broadcast(list(src.shape)), ALU.mult)

            def spread(row, n):
                return row[:, :].rearrange("p (o c) -> p o c", o=1).to_broadcast([P, n, C])

            pool.sem_inc(cparts_done, 1)
            pool.sem_inc(cparts_out, 3 * 16)
            pool.sem_inc(xd_free, 1)
            pool.sem_inc(rows_added, 2)
            link(pool.memset(held_p[:, 9:10], 1.0))
            link(pool.memset(ident[:, :], 0.0))
            pool.affine_select(out=ident[:, :], in_=ident[:, :], compare_op=ALU.not_equal, fill=1.0, base=0,
                               pattern=[[-1, P]], channel_multiplier=1).then_inc(consts_done, 1)

            link(pool.memset(ones[:, :], 1.0))
            pool.affine_select(out=below[:, :], in_=ones[:, :], compare_op=ALU.is_gt, fill=0.0, base=0,
                               pattern=[[1, P]], channel_multiplier=-1)
            pool.iota(iota_e[:, :], pattern=[[1, E]], base=0, channel_multiplier=0,
                      allow_small_or_imprecise_dtypes=True)
            pool.iota(slot_base[:, :, :], pattern=[[CAP, TOPK], [SLOTS, E]], base=0, channel_multiplier=0,
                      allow_small_or_imprecise_dtypes=True)
            pool.iota(token_no[:, :], pattern=[[P, B * QT]], base=0, channel_multiplier=1,
                      allow_small_or_imprecise_dtypes=True)
            pool.memset(carry[:, :], 0.0)
            link(pool.memset(empty[:, :], 0.0))
            pool.memset(empty[:, C + TOPK:ROW], float(NOBODY)).then_inc(empty_done, 1)

            def batch(b):
                pool.wait_ge(ctxk_in, (b + 1) * 16)
                pool.wait_ge(cparts_out, (b + 1) * (3 * 16))
                link(copy(c_parts[:, 0], ctxk[:, :, :]))
                link(pool.tensor_tensor(ctxk[:, :, :], ctxk[:, :, :], c_parts[:, 0], ALU.subtract))
                link(copy(c_parts[:, 1], ctxk[:, :, :]))
                pool.tensor_tensor(c_parts[:, 2], ctxk[:, :, :], c_parts[:, 1], ALU.subtract) \
                    .then_inc(cparts_done, 1)

            pv, turn, rt = Tally(), Tally(), Tally()

            def set_v(b, g):
                for half in range(2):
                    ins = copy(
                        v_ones[:, half * QT:(half + 1) * QT, HG * g:HG * (g + 1), 0:D],
                        v_stash[:, half, bass.ds(b, 1), :, HG * D * g:HG * D * (g + 1)]
                        .rearrange("p o t (h d) -> p (o t) h d", d=D))
                ins.then_inc(v_set, 1)

            def cut_max():
                pool.wait_ge(misc_free, turn.at())
                link(copy(neg_parts[:, 0, :], neg_m[:, :]))
                link(pool.tensor_tensor(neg_m[:, :], neg_m[:, :], neg_parts[:, 0, :], ALU.subtract))
                link(copy(neg_parts[:, 1, :], neg_m[:, :]))
                pool.tensor_tensor(neg_parts[:, 2, :], neg_m[:, :], neg_parts[:, 1, :], ALU.subtract) \
                    .then_inc(shift_done, 1)

            with pool.Fori(0, B - 1) as b:
                link_n.begin(b, 3)
                batch(b)
                link_n.end(B - 1)
            pool.memset(v_ones[:, :, :, D:2 * D], 1.0).then_inc(consts_done, 1)
            pool.wait_ge(vctx_in, 16)
            pool.wait_ge(qkv_out, 6 + 2)
            for g in range(G):
                set_v(0, g)
            batch(B - 1)
            pool.wait_ge(gates_done, 1)
            pool.wait_ge(consts_in, 4 * 16)
            pool.tensor_scalar(bias_row[:, :], bias_row[:, :], tanh_g[:, 1:2], None, ALU.mult)
            link(pool.tensor_scalar(b_row[:, :], b_row[:, :], tanh_g[:, 0:1], None, ALU.mult))
            pool.wait_ge(xn_done, B)
            pool.tensor_tensor(x_sb[:, :, :], x_sb[:, :, :], spread(b_row, B * QT), ALU.add).then_inc(xb_done, 1)
            pool.wait_ge(qkv_out, 6 * B + 2)
            turn.step()
            cut_max()

            def cut_w1(n, k):
                for j, (lo, raw, hi) in enumerate(zip(pieces(w1_p[k][1]), pieces(w1_raw[k]), pieces(w1_p[k][0]))):
                    pool.wait_ge(w_hi, n * 4 + (j + 1))
                    pool.tensor_tensor(lo, raw, hi, ALU.subtract).then_inc(w1_lo, 1)

            def steps(c0, c1, i=0):
                for c in range(c0, c1):
                    for what, n in steps_at(c):
                        if what in SHARED:
                            turn.step()
                        if what == "norm2" and c >= STEPS:
                            cut_w1(0, 0)
                        if what == "values":
                            pv.step()
                        elif what == "set_v":
                            pool.wait_ge(pv_done, pv.at(-1 - 2 * KT))
                            set_v(i + n // G, n % G)
                        elif what == "turn_max":
                            pool.wait_ge(shift_in[(n - 1) % G], (i + ((n - 1) // G + 1)) * (16 * NPART))
                            cut_max()
                        elif what == "scatter":
                            rt.step()
                            pool.wait_ge(empty_out, 2 * 16)
                            pool.wait_ge(slot_done, rt.at())
                            hold(0)
                            for t in range(QT):
                                for k in range(TOPK):
                                    pool.indirect_dma_start(
                                        out=slot_dram, out_offset=bass.IndirectOffsetOnAxis(
                                            ap=slot_u[:, t, k:k + 1], axis=0),
                                        in_=xd[:, t, :], in_offset=None,
                                        bounds_check=NSLOT - 1, oob_is_err=False).then_inc(scattered, 16)
                            pool.wait_ge(xd_done, rt.at())
                            rows = x_sb[:, bass.ds(i * QT + n * QT, QT), :]
                            pool.tensor_tensor(rows, rows, spread(bias_row, QT), ALU.add).then_inc(res_done, 1)
                            pool.wait_ge(res_done, rt.at())
                            hold(1)
                            pool.dma_start(out[bass.ds(i * T + n * T, T), :].rearrange("(q p) c -> p q c", p=P),
                                           rows).then_inc(res_out, 16)
                            pool.wait_ge(scattered, rt.at() * (QT * TOPK * 16))
                            touch(2).then_inc(xd_free, 1)

            run_steps(pool, steps, [(pv, G * KT), (turn, TURNS), (rt, 1), (link_n, 3 * G + 2)])

            def add_rows(n, k):
                pool.wait_ge(tok_done, n + 1)
                link(touch(8))
                for s in range(SPE):
                    pool.wait_ge(y_done, n * SPE + (s + 3))
                    hold(3 + s)
                    pool.indirect_dma_start(
                        out=out, out_offset=bass.IndirectOffsetOnAxis(ap=tok_u[k][:, s:s + 1], axis=0),
                        in_=y_sb[k][:, s, :], in_offset=None, bounds_check=NTOK - 1, oob_is_err=False,
                        compute_op=ALU.add).then_inc(added, 16)
                pool.wait_ge(added, n * (SPE * 16) + SPE * 16)
                touch(7).then_inc(rows_added, 1)

            pool.wait_ge(res_out, B * 16)
            with pool.Fori(0, (E - 2) // 2) as j:
                link_n.begin(j, 2 * (SPE + 1))
                cut_w1(j * 2 + 1, 1)
                add_rows(j * 2, 0)
                cut_w1(j * 2 + 2, 0)
                add_rows(j * 2 + 1, 1)
                link_n.end((E - 2) // 2)
            cut_w1(E - 1, 1)
            add_rows(E - 2, 0)
            add_rows(E - 1, 1)

        @block.scalar
        def _(act):
            act.sem_inc(qkv_out, 6)
            act.sem_inc(h_out, 4)
            act.wait_ge(gate_in, 32)
            act.activation(tanh_g[:, :], gates[:, :], ACT.Tanh).then_inc(gates_done, 1)
            st, kt_n, turn, oc, rt, tmax = (Tally() for _ in range(6))

            def evict(dst, scale=1.0, src=MISC):
                turn.step()
                act.wait_ge(misc_ready, turn.at())
                return act.activation(dst, src, ACT.Copy, scale=scale).then_inc(misc_free, 1)

            def cut_high(n, k):
                act.wait_ge(w_raw_in[k], (n - k) * 16 + 32)
                for raw, part in ((w1_raw, w1_p), (w2_raw, w2_p)):
                    for hi, src in zip(pieces(part[k][0]), pieces(raw[k])):
                        act.activation(hi, src, ACT.Copy).then_inc(w_hi, 1)

            def turn_max():
                tmax.step()
                evict(neg_m[:, :], -1.0, MISC[0:SLOTS_PER_GROUP, 0:P])

            def project(b, last=False):
                for k in range(2):
                    act.wait_ge(xnT_ready, b * 2 + (k + 1))
                    act.activation(xnT[:, k, :], bank(6 + k), ACT.Copy).then_inc(xnT_done, 1)
                for j in range(2):
                    act.wait_ge(qkv_ready, b * 6 + (j + 1))
                    act.activation(v_stash[:, 1, bass.ds(b, 1), 2 * j:2 * j + 2, :].rearrange("p o t c -> p (o t c)"),
                                   bank(6 + j), ACT.Copy).then_inc(qkv_out, 1)
                for m in range(4):
                    if m % 2 == 0:
                        act.wait_ge(parts_done, b * 2 + (m // 2 + 1))
                        act.wait_ge(parts_out[m // 2], (b + 1) * (3 * 16))
                    act.wait_ge(qkv_ready, b * 6 + (m + 3))
                    scale = D ** -0.5 if m < 2 else 1.0
                    act.activation(qk[:, m, :], bank(4 + m % 2), ACT.Copy, scale=scale)
                    act.activation(parts[:, 0, m, :], bank(4 + m % 2), ACT.Copy, scale=scale).then_inc(qkv_out, 1)
                    if last and m == 2:
                        turn_max()

            with act.Fori(0, B - 1) as b:
                project(b)
            project(B - 1, last=True)

            def steps(c0, c1, i=0):
                for c in range(c0, c1):
                    for what, n in steps_at(c):
                        if what == "scores":
                            kt, pair = c % SLOTS_PER_GROUP // 2, c % 2
                            buf = pexp[kt % NP]
                            if pair == 0:
                                kt_n.step()
                                if c >= 2 * NP:
                                    act.wait_ge(pv_done, kt_n.at(-NP))
                            for j in range(2):
                                st.step()
                                act.wait_ge(st_ready, st.at())
                                act.activation(buf[:, 2 * pair + j, :], bank(4 + j), ACT.Exp).then_inc(exp_done, 1)
                        elif what == "copy_out":
                            oc.step()
                            act.wait_ge(pv_done, oc.at() * KT)
                            act.wait_ge(misc_ready, turn.at())
                            act.activation(o_t[:, :], bank(6), ACT.Copy).then_inc(o_copied, 1)
                        elif what == "turn_max":
                            act.wait_ge(shift_done, tmax.at())
                            turn_max()
                        elif what in ("attn_t0", "attn_t1"):
                            evict(o_natT[:, int(what[-1]), :])
                        elif what in ("x1_t0", "x1_t1"):
                            evict(x1T[:, int(what[-1]), :])
                        elif what in SHARED:
                            turn.step()
                        elif what == "top2":
                            rt.step()
                            act.wait_ge(misc_free, turn.at())
                            act.activation(lexp[:, :, :], lshift[:, :, :], ACT.Exp).then_inc(lexp_done, 1)
                        if what == "proj0" and c >= STEPS:
                            cut_high(0, 0)

            act.wait_ge(parts_done, 2 * B + 2)
            act.wait_ge(cparts_done, B + 1)
            run_steps(act, steps, [(st, 2 * PERIOD), (kt_n, G * KT), (turn, TURNS), (oc, G), (rt, 1), (tmax, G)])

            def hidden(n):
                for f in range(FT):
                    act.wait_ge(h_ready, n * FT + (f + 1))
                    act.wait_ge(hid_done, n * FT + (f + 1))
                    act.activation(hid[:, f % 4, :], bank(2 + f % 4), ACT.Gelu_apprx_tanh).then_inc(h_out, 1)
                    act.wait_ge(h_out, n * FT + (f + 5))
                    act.activation(hid_p[0][:, f, :], hid[:, f % 4, :], ACT.Copy).then_inc(hhi_done, 1)

            hidden(0)
            with act.Fori(0, (E - 2) // 2) as j:
                cut_high(j * 2 + 1, 1)
                hidden(j * 2 + 1)
                cut_high(j * 2 + 2, 0)
                hidden(j * 2 + 2)
            cut_high(E - 1, 1)
            hidden(E - 1)

        @block.vector
        def _(dve):
            link_n = Tally()

            def link(ins):
                ins.then_inc(chain_v, 1)
                link_n.step()
                dve.wait_ge(chain_v, link_n.at())

            def hold():
                dve.tensor_copy(held[:, 0:1], held[:, 1:2]).then_inc(chain_v, 1)
                link_n.step()

            def x_row(b, t):
                return x_sb[:, bass.ds(b * QT + t, 1), :].rearrange("p o c -> p (o c)")

            def layer_norm(dst, b, done):
                hold()
                for t in range(QT):
                    ins = dve.bn_stats(stats[:, t, :], x_row(b, t))
                link(ins)
                hold()
                for t in range(QT):
                    ins = dve.bn_aggr(meanvar[:, t, :], stats[:, t, :])
                link(ins)
                link(dve.tensor_scalar(var[:, :], meanvar[:, :, 1], EPS, None, ALU.add))
                link(dve.tensor_scalar(rstd[:, :].bitcast(I32), var[:, :].bitcast(I32), -0.5, ROOT_SEED,
                                       ALU.mult, ALU.add))
                for _ in range(NEWTON):
                    link(dve.scalar_tensor_tensor(out=root_t[:, :], in0=rstd[:, :], scalar=-0.5, in1=rstd[:, :],
                                                  op0=ALU.mult, op1=ALU.mult))
                    link(dve.tensor_tensor(root_t[:, :], root_t[:, :], var[:, :], ALU.mult))
                    link(dve.scalar_tensor_tensor(out=rstd[:, :], in0=root_t[:, :], scalar=1.5, in1=rstd[:, :],
                                                  op0=ALU.add, op1=ALU.mult))
                for t in range(QT):
                    ins = dve.tensor_scalar(dst[:, t, 0:C], x_row(b, t), meanvar[:, t, 0:1],
                                            rstd[:, t:t + 1], ALU.subtract, ALU.mult)
                ins.then_inc(done, 1)

            def cut(b, half):
                dve.wait_ge(qkv_out, b * 6 + (10 + 2 * half))
                x, part = qk[:, 2 * half:2 * half + 2, :], parts[:, :, 2 * half:2 * half + 2, :]
                link(dve.tensor_tensor(x, x, part[:, 0], ALU.subtract))
                link(dve.tensor_copy(part[:, 1], x))
                dve.tensor_tensor(part[:, 2], x, part[:, 1], ALU.subtract).then_inc(parts_done, 1)

            unit, turn, rt = Tally(), Tally(), Tally()

            def row_max(u):
                unit.step()
                dve.wait_ge(s_ready, unit.at())
                group, j = u // SLOTS_PER_GROUP, u % SLOTS_PER_GROUP
                dve.reduce_max(mx[:, group % 2, j:j + 1], bank(2 * (u % 2), 2).rearrange("p a t -> p (a t)"),
                               AX_X).then_inc(max_done, 1)

            def next_batch(b):
                dve.wait_ge(xnT_ready, (b + 1) * 2)
                layer_norm(xn, b + 1, xn_done)

            dve.sem_inc(parts_done, 2)
            dve.sem_inc(hid_done, 4)
            dve.sem_inc(y_done, 2)
            dve.memset(k6[KROWS:P, 0:1, :], 1.0).then_inc(one_row, 1)
            link(dve.memset(held[:, :], 0.0))
            dve.wait_ge(x0_in, 16)
            layer_norm(xn, 0, xn_done)
            dve.wait_ge(x_in_s, 16)
            with dve.Fori(0, B - 2) as b:
                link_n.begin(b, NORM_LINKS + 4)
                next_batch(b)
                cut(b, 0)
                cut(b, 1)
                link_n.end(B - 2)
            for b, counts in UNITS_AFTER.items():
                if b + 1 < B:
                    next_batch(b)
                for point, count in enumerate(counts):
                    for _ in range(count):
                        row_max(unit.n)
                    if point in (2, 4):
                        cut(b, point // 2 - 1)

            def wait_turn():
                turn.step()
                dve.wait_ge(misc_ready, turn.at())

            def per_row(x, n, shape):
                return x.rearrange("p (q o) -> p q o", o=1).to_broadcast(shape)

            def steps(c0, c1, i=0):
                for c in range(c0, c1):
                    for what, n in steps_at(c):
                        if what == "max":
                            row_max(n)
                        elif what == "turn_out":
                            wait_turn()
                            o4 = MISC.rearrange("p (q h d) -> p q h d", q=QT, h=HG)
                            link(dve.reciprocal(rden[:, :, :], o4[:, :, :, D]))
                            g = n % G
                            dve.tensor_tensor(
                                o_nat[:, :, HG * D * g:HG * D * (g + 1)].rearrange("p q (h d) -> p q h d", d=D),
                                o4[:, :, :, 0:D],
                                rden[:, :, :].rearrange("p q (h o) -> p q h o", o=1).to_broadcast([P, QT, HG, D]),
                                ALU.mult).then_inc(misc_free, 1)
                        elif what in ("proj0", "proj1"):
                            wait_turn()
                            j = int(what[-1])
                            rows = x_sb[:, bass.ds((i + n) * QT + 2 * j, 2), :].rearrange("p o c -> p (o c)")
                            dve.wait_ge(xb_done, 1)
                            dve.scalar_tensor_tensor(out=rows, in0=MISC, scalar=tanh_g[:, 0:1], in1=rows,
                                                     op0=ALU.mult, op1=ALU.add).then_inc(misc_free, 1)
                        elif what == "norm2":
                            dve.wait_ge(misc_free, turn.at())
                            rt.step()
                            dve.wait_ge(xd_free, rt.at())
                            layer_norm(xd, i + n, x1_done)
                        elif what == "router":
                            wait_turn()
                            lg = MISC[:, 0:QT * E].rearrange("p (q e) -> p q e", e=E)
                            link(dve.tensor_reduce(lmax[:, :], lg, AX_X, ALU.max))
                            dve.tensor_tensor(lshift[:, :, :], lg, per_row(lmax[:, :], E, [P, QT, E]),
                                              ALU.subtract).then_inc(misc_free, 1)
                        elif what == "top2":
                            dve.wait_ge(lexp_done, rt.at())
                            link(dve.tensor_reduce(lsum[:, :], lexp[:, :, :], AX_X, ALU.add))
                            link(dve.reciprocal(lsum[:, :], lsum[:, :]))
                            link(dve.tensor_tensor(score[:, :, :], lexp[:, :, :],
                                                   per_row(lsum[:, :], E, [P, QT, E]), ALU.mult))
                            hold()
                            for t in range(QT):
                                ins = dve.max(top[:, t, :], score[:, t, :])
                            link(ins)
                            hold()
                            for t in range(QT):
                                ins = dve.max_index(top_e[:, t, :], top[:, t, :], score[:, t, :])
                            link(ins)
                            link(dve.tensor_copy(top_ef[:, :, :], top_e[:, :, 0:TOPK]))
                            for k in range(TOPK):
                                ins = dve.tensor_tensor(
                                    hot[:, :, k * E:(k + 1) * E],
                                    iota_e[:, :].rearrange("p (o e) -> p o e", o=1).to_broadcast([P, QT, E]),
                                    per_row(top_ef[:, :, k], E, [P, QT, E]), ALU.is_equal)
                            ins.then_inc(hot_done, 1)
                            dve.tensor_scalar(xd[:, :, C:C + TOPK], top[:, :, 0:TOPK], tanh_g[:, 1:2], None, ALU.mult)
                            dve.tensor_copy(xd[:, :, C + TOPK:ROW].rearrange("p q o -> p (q o)"),
                                            token_no[:, bass.ds((i + n) * QT, QT)]).then_inc(xd_done, 1)
                        elif what == "ranks":
                            wait_turn()
                            rk = MISC[:, 0:QT * TOPK * E].rearrange("p (q n) -> p q n", n=TOPK * E)
                            base = slot_base[:, :, :].rearrange("p (o k) e -> p o (k e)", o=1) \
                                .to_broadcast([P, QT, TOPK * E])
                            dve.tensor_tensor(pos[:, :, :], rk, base, ALU.add)
                            dve.tensor_scalar(over[:, :, :], rk, float(CAP), float(DROPPED), ALU.is_ge, ALU.mult) \
                                .then_inc(misc_free, 1)
                            link(dve.tensor_reduce(hot_sum[:, :], hot[:, :, :].rearrange("p q n -> p n q"),
                                                   AX_X, ALU.add))
                            dve.wait_ge(misc_free, turn.at())
                            dve.tensor_tensor(carry[:, :], carry[:, :], hot_sum[:, :], ALU.add)
                            link(dve.tensor_tensor(pos[:, :, :], pos[:, :, :], over[:, :, :], ALU.add))
                            link(dve.tensor_tensor(pos[:, :, :], pos[:, :, :], hot[:, :, :], ALU.mult))
                            link(dve.tensor_reduce(slot_f[:, :, :], pos[:, :, :].rearrange("p q (k e) -> p q k e", e=E),
                                                   AX_X, ALU.add))
                            dve.tensor_copy(slot_u[:, :, :], slot_f[:, :, :]).then_inc(slot_done, 1)
                        elif what in SHARED:
                            turn.step()
                        if what == "x1_t1" and c >= STEPS:
                            cut_w2(0, 0, 0)
                            cut_w2(0, 0, 1)

            def cut_w2(n, k, j):
                dve.wait_ge(w_hi, n * 4 + (j + 3))
                dve.tensor_tensor(pieces(w2_p[k][1])[j], pieces(w2_raw[k])[j], pieces(w2_p[k][0])[j],
                                  ALU.subtract).then_inc(w2_lo, 1)

            turn.step()
            run_steps(dve, steps, [(unit, PERIOD), (turn, TURNS), (rt, 1),
                                   (link_n, G + NORM_LINKS + 1 + 8 + 4)])

            def cut_rows(n, k):
                for c in range(2):
                    dve.wait_ge(xeT_ready, n * 2 + (c + 1))
                    link(dve.tensor_copy(xeT[0][:, c, :], bank(c)))
                    dve.tensor_tensor(xeT[1][:, c, :], bank(c), xeT[0][:, c, :], ALU.subtract).then_inc(xeT_done, 1)
                dve.wait_ge(rows_added, n + 1)
                dve.tensor_copy(tok_u[k][:, :], xe[k][:, :, ROW - 1]).then_inc(tok_done, 1)

            def results(n, k):
                for s in range(SPE):
                    dve.wait_ge(y_ready, n * SPE + (s + 1))
                    w = C + s * P // CAP
                    dve.tensor_scalar(y_sb[k][:, s, :], bank(6 + s % 2)[:, 0:C], xe[k][:, s, w:w + 1], None,
                                      ALU.mult).then_inc(y_done, 1)

            def hidden(n, k, first=False):
                for f in range(FT):
                    dve.wait_ge(hhi_done, n * FT + (f + 1))
                    dve.tensor_tensor(hid_p[1][:, f, :], hid[:, f % 4, :], hid_p[0][:, f, :], ALU.subtract) \
                        .then_inc(hid_done, 1)
                    if f in (1, 3) and not first:
                        cut_w2(n, k, f // 2)

            cut_rows(0, 0)
            hidden(0, 0, first=True)

            def expert(n, k):
                cut_rows(n, k)
                results(n - 1, 1 - k)
                hidden(n, k)

            with dve.Fori(0, (E - 2) // 2) as j:
                link_n.begin(j, 4)
                expert(j * 2 + 1, 1)
                expert(j * 2 + 2, 0)
                link_n.end((E - 2) // 2)
            expert(E - 1, 1)
            results(E - 1, 1)

        @block.tensor
        def _(pe):
            pe.wait_ge(w_in, 16)
            pe.wait_ge(consts_done, 1)
            unit, st, pv, turn, group, rt = (Tally() for _ in range(6))

            def max_scores(u, i=0):
                g, j = u // SLOTS_PER_GROUP, u % SLOTS_PER_GROUP
                head, qt = g % G * HG + j // QT, j % QT
                if j == 0:
                    pe.wait_ge(qk_in[g % G], (i + (g // G + 1)) * (2 * 16 * len(PAIRS)))
                if u >= 2:
                    pe.wait_ge(max_done, unit.at(-1))
                for half in range(2):
                    mm = pe.matmul(bank(2 * (u % 2) + half), q6[0:KROWS, head, qt * P:(qt + 1) * P],
                                   k6[0:KROWS, head, half * 512:(half + 1) * 512], start=True, stop=True)
                mm.then_inc(s_ready, 1)
                unit.step()

            def take_turn(u=None):
                if u is None:
                    pe.wait_ge(misc_free, turn.at())
                turn.step()

            def turn_max(g, first=False):
                pe.wait_ge(max_done, group_units(g))
                take_turn(0 if first else None)
                pe.transpose(MISC[0:SLOTS_PER_GROUP, 0:P], mx[:, g % 2, :], ident[:, :]).then_inc(misc_ready, 1)

            tm = Tally()

            def group_units(g):
                tm.step()
                return tm.at() * SLOTS_PER_GROUP

            def project(b, counts=()):
                def units(point):
                    if counts:
                        for _ in range(counts[point]):
                            max_scores(unit.n)

                pe.wait_ge(xn_done, b + 1)
                pe.wait_ge(qkv_out, b * 6 + 2)
                for k in range(2):
                    for t in range(QT):
                        mm = pe.transpose(bank(6 + k)[:, t * P:(t + 1) * P], xn[:, t, k * P:(k + 1) * P], ident[:, :])
                    mm.then_inc(xnT_ready, 1)
                pe.wait_ge(xnT_done, b * 2 + 2)
                for j in range(2):
                    for t in range(2):
                        for k in range(2):
                            mm = pe.matmul(bank(6 + j)[:, t * C:(t + 1) * C],
                                           xnT[:, k, (2 * j + t) * P:(2 * j + t + 1) * P], w_qkv[:, k, 2 * C:3 * C],
                                           start=(k == 0), stop=(k == 1))
                    mm.then_inc(qkv_ready, 1)
                units(0)
                for m in range(4):
                    pe.wait_ge(qkv_out, b * 6 + (5 + m + 2 * (m // 2)))
                    for k in range(2):
                        mm = pe.matmul(bank(4 + m % 2), w_qkv[:, k, m * P:(m + 1) * P], xnT[:, k, :],
                                       start=(k == 0), stop=(k == 1))
                    mm.then_inc(qkv_ready, 1)
                    units(m + 1)
                    if m == 2 and len(counts) and b == B - 1:
                        turn_max(0, first=True)

            with pe.Fori(0, B - 2) as b:
                project(b)
            pe.wait_ge(k_ones, 16)
            for b, counts in UNITS_AFTER.items():
                project(b, counts)
            pe.wait_ge(qkv_out, 6 * (B + 1))

            def steps(c0, c1, i=0):
                for c in range(c0, c1):
                    s = c % SLOTS_PER_GROUP
                    for what, n in steps_at(c):
                        if what == "max":
                            max_scores(n, i)
                        elif what == "scores":
                            g, kt, pair = c // SLOTS_PER_GROUP, s // 2, s % 2
                            if s == 0:
                                pe.wait_ge(shift_in[g % G], (i + (g // G + 1)) * (16 * NPART))
                            for j in range(2):
                                head = g % G * HG + 2 * pair + j
                                if c >= 1:
                                    pe.wait_ge(exp_done, st.at(-1))
                                pe.matmul(bank(4 + j), k6[0:AROWS, head, kt * P:(kt + 1) * P], q6[0:AROWS, head, :],
                                          start=True, stop=True).then_inc(st_ready, 1)
                                st.step()
                        elif what == "values":
                            g = (c - 1) // SLOTS_PER_GROUP
                            if n == 0:
                                group.step()
                                pe.wait_ge(v_set, group.at())
                                if c >= SLOTS_PER_GROUP:
                                    pe.wait_ge(o_copied, group.at(-1))
                            pv.step()
                            pe.wait_ge(exp_done, pv.at() * HG)
                            for j in range(HG):
                                mm = pe.matmul(bank(6)[j * 2 * D:(j + 1) * 2 * D, :],
                                               v_ones[:, n, g % G * HG + j, :], pexp[n % NP][:, j, :],
                                               start=(n == 0), stop=(n == KT - 1))
                            mm.then_inc(pv_done, 1)
                        elif what == "turn_out":
                            pe.wait_ge(o_copied, group.at(to_out(c)))
                            take_turn()
                            for q in range(QT):
                                mm = pe.transpose(MISC[:, q * P:(q + 1) * P], o_t[:, q * P:(q + 1) * P], ident[:, :])
                            mm.then_inc(misc_ready, 1)
                        elif what == "turn_max":
                            turn_max(n)
                        elif what in ("attn_t0", "attn_t1", "x1_t0", "x1_t1"):
                            k = int(what[-1])
                            take_turn()
                            if what == "attn_t0":
                                rt.step()
                            if what == "x1_t0":
                                pe.wait_ge(x1_done, rt.at())
                            src = o_nat if what[0] == "a" else xd
                            for q in range(QT):
                                mm = pe.transpose(MISC[:, q * P:(q + 1) * P], src[:, q, k * P:(k + 1) * P], ident[:, :])
                            mm.then_inc(misc_ready, 1)
                        elif what in ("proj0", "proj1"):
                            j = int(what[-1])
                            take_turn()
                            pe.wait_ge(consts_in, 4 * 16)
                            for t in range(2):
                                for k in range(2):
                                    mm = pe.matmul(MISC[:, t * C:(t + 1) * C],
                                                   o_natT[:, k, (2 * j + t) * P:(2 * j + t + 1) * P], w_p[:, k, :],
                                                   start=(k == 0), stop=(k == 1))
                            mm.then_inc(misc_ready, 1)
                        elif what == "router":
                            take_turn()
                            for t in range(QT):
                                for k in range(2):
                                    mm = pe.matmul(MISC[:, t * E:(t + 1) * E], x1T[:, k, t * P:(t + 1) * P],
                                                   w_r[:, k, :], start=(k == 0), stop=(k == 1))
                            mm.then_inc(misc_ready, 1)
                        elif what == "ranks":
                            take_turn()
                            pe.wait_ge(hot_done, rt.at())
                            n16 = TOPK * E
                            for t in range(QT):
                                dst = MISC[:, t * n16:(t + 1) * n16]
                                pe.matmul(dst, below[:, :], hot[:, t, :], start=True, stop=False)
                                for before in range(t):
                                    pe.matmul(dst, ones[:, :], hot[:, before, :], start=False, stop=False)
                                mm = pe.matmul(dst, ones[:, :], carry[:, :], start=False, stop=True)
                            mm.then_inc(misc_ready, 1)

            def to_out(c):
                return -1 if c < STEPS else 0

            run_steps(pe, steps, [(unit, PERIOD), (st, 2 * PERIOD), (pv, G * KT), (turn, TURNS), (group, G),
                                  (rt, 1), (tm, G)])

            def rows(n, k):
                pe.wait_ge(xe_in[k], (n - k) * 8 + 16)
                for c in range(2):
                    for s in range(SPE):
                        mm = pe.transpose(bank(c)[:, s * P:(s + 1) * P], xe[k][:, s, c * P:(c + 1) * P], ident[:, :])
                    mm.then_inc(xeT_ready, 1)

            PASSES = [(0, 0), (0, 1), (1, 0)]

            def hidden(n, k):
                pe.wait_ge(w1_lo, n * 2 + 2)
                pe.wait_ge(xeT_done, (n + 1) * 2)
                for f in range(FT):
                    pe.wait_ge(h_out, n * FT + (f + 1))
                    terms = [(c, a, b) for c in range(2) for a, b in PASSES]
                    for c, a, b in terms:
                        mm = pe.matmul(bank(2 + f % 4), w1_p[k][a][:, c, f * P:(f + 1) * P], xeT[b][:, c, :],
                                       start=(c, a, b) == terms[0], stop=(c, a, b) == terms[-1])
                    mm.then_inc(h_ready, 1)

            def results(n, k):
                pe.wait_ge(w2_lo, n * 2 + 2)
                for s in range(SPE):
                    pe.wait_ge(y_done, n * SPE + (s + 1))
                    terms = [(f, a, b) for f in range(FT) for a, b in PASSES]
                    for f, a, b in terms:
                        if s == 0 and (a, b) == PASSES[0]:
                            pe.wait_ge(hid_done, n * FT + (f + 5))
                        mm = pe.matmul(bank(6 + s % 2)[:, 0:C], hid_p[a][:, f, s * P:(s + 1) * P], w2_p[k][b][:, f, :],
                                       start=(f, a, b) == terms[0], stop=(f, a, b) == terms[-1])
                    mm.then_inc(y_ready, 1)

            rows(0, 0)
            hidden(0, 0)
            with pe.Fori(0, (E - 2) // 2) as j:
                rows(j * 2 + 1, 1)
                results(j * 2, 0)
                hidden(j * 2 + 1, 1)
                rows(j * 2 + 2, 0)
                results(j * 2 + 1, 1)
                hidden(j * 2 + 2, 0)
            rows(E - 1, 1)
            results(E - 2, 0)
            hidden(E - 1, 1)
            results(E - 1, 1)


_OUT = ((B, T, C), "float32")


def kernel(**inputs):
    import concourse.bacc as _bacc
    import numpy as _np
    from concourse.bass_utils import run_bass_kernel_spmd as _run

    a = {k: _np.asarray(v) for k, v in inputs.items()}
    ctx = a["ctx_2048"]
    arrays = {
        "x": a["x"].reshape(NTOK, C),
        "ctx_kT": ctx[:, :, 0:C].transpose(0, 2, 1),
        "ctx_v": ctx[:, :, C:2 * C],
        "g_xattn": a["g_xattn"].reshape(1, 1),
        "g_ffn": a["g_ffn"].reshape(1, 1),
        "w_qkvT": a["L0_xattn_w_qkv"].T,
        "w_projT": a["L0_xattn_w_proj"].T,
        "b_proj": a["L0_xattn_b_proj"].reshape(1, C),
        "router_w": a["L0_ffn_router_w"],
        "w1": a["L0_ffn_w1"],
        "w2": a["L0_ffn_w2"],
        "bias": a["L0_ffn_bias"].reshape(1, C),
    }
    arrays = {k: _np.ascontiguousarray(v) for k, v in arrays.items()}
    nc = _bacc.Bacc("TRN2", target_bir_lowering=False, num_devices=1)
    args = [nc.dram_tensor(k, v.shape, mybir.dt.from_np(v.dtype), kind="ExternalInput").ap()
            for k, v in arrays.items()]
    args.append(nc.dram_tensor("out", (NTOK, C), F32, kind="ExternalOutput").ap())
    build(nc, *args)
    r = _run(nc, [arrays], core_ids=[0])
    return r.results[0]["out"].reshape(_OUT[0])
```

```python
from contextlib import ExitStack

import concourse.bass as bass
from concourse import mybir

ALU = mybir.AluOpType
ACT = mybir.ActivationFunctionType
F32 = mybir.dt.float32
F32R = mybir.dt.float32r
BF16 = mybir.dt.bfloat16
U32 = mybir.dt.uint32
I32 = mybir.dt.int32
AX_X = mybir.AxisListType.X

P = 128
B, T, C = 4, 512, 256
H, D = 16, 16
TC = 512
NKEY = TC + T
KT = NKEY // P
QT = T // P
G, HG = 4, 4
NGROUP = B * G
E, F, TOPK = 8, 1024, 2
EW = 32
NTOK = B * T
CAP = NTOK // E
SLOTS = TOPK * CAP
NSLOT = E * SLOTS
ROW = C + TOPK + 1
NPART = 3
PAIRS = [(0, 0), (0, 1), (0, 2), (1, 0), (1, 1), (2, 0)]
KROWS = len(PAIRS) * D
AROWS = KROWS + NPART
EPS = 1e-5
ROOT_SEED = 1597463007.0
NEWTON = 3
NORM_LINKS = 8 + 3 * NEWTON
NOBODY = 1 << 20
DROPPED = 1 << 16

SLOTS_PER_GROUP = 16
STEPS = NGROUP * SLOTS_PER_GROUP
PERIOD = G * SLOTS_PER_GROUP
LEAD = 24
TURN = PERIOD - LEAD
UNITS_AFTER = {B - 2: (2, 2, 2, 2, 2), B - 1: (2, 2, 2, 4, 4)}
NP = 4


def steps_at(c):
    s, p, g = c % SLOTS_PER_GROUP, c % PERIOD, c // SLOTS_PER_GROUP
    behind = 1 <= g <= NGROUP
    late = int(c > STEPS - LEAD + 1)
    if behind and s == 1 + late:
        yield "copy_out", g - 1
    if c < STEPS:
        yield "scores", c
    if 2 <= c <= STEPS + 1 and s % 2 == late:
        yield "values", (s // 2 - 1) % KT
    if s % 2 and c + LEAD < STEPS:
        yield "max", c + LEAD - 1
        yield "max", c + LEAD
    if behind and s == 1 and g + 3 < NGROUP:
        yield "load", g + 3
    if s == 2 and g >= 3 and g + 1 < NGROUP:
        yield "set_v", g + 1
    if behind and s == 5:
        yield "turn_out", g - 1
    if s == 10 and g + 1 < NGROUP:
        yield "turn_max", g + 1
    for name in (LAST_ROUTE_AT if c >= STEPS else ROUTE_AT).get(p, []) if c >= PERIOD else []:
        yield name, c // PERIOD - 1
    if c in LAST_EARLY:
        yield LAST_EARLY[c], B - 1


ROUTE_AT = {7: ["attn_t0"], 8: ["attn_t1"], 9: ["proj0"], 10: ["stats0"], 11: ["proj1"],
            12: ["stats1"], 13: ["variance"], 14: ["newton"], 15: ["newton"], 16: ["newton"], 17: ["norm0"],
            18: ["norm1"], 20: ["x1_t0"], 22: ["x1_t1"], 23: ["router"], 24: ["router_t"], 25: ["softmax", "top2"],
            26: ["expert_of"], 29: ["ranks"], 30: ["scatter"]}
assert sum(step == ["newton"] for step in ROUTE_AT.values()) == NEWTON
LAST_EARLY = {STEPS - 23: "last_t0", STEPS - 19: "last_proj0", STEPS + 2: "last_proj_2", STEPS + 6: "last_proj_3"}
LAST_ROUTE_AT = {7: ["last_t1"], 8: ["last_proj1", "variance"] + ["newton"] * NEWTON + ["norm0", "norm1"],
                 9: ["last_x1_t"], 10: ["router", "router_t", "softmax", "top2", "expert_of", "ranks", "scatter"]}
SHARED = ("last_t0", "last_t1", "turn_out", "turn_max", "attn_t0", "attn_t1", "proj0", "proj1", "x1_t0",
          "x1_t1", "router", "router_t",
          "ranks")
TURNS = 2 * G + 9


class Tally:

    def __init__(self):
        self.n, self.reg, self.per = 0, None, 0

    def step(self, m=1):
        self.n += m

    def at(self, d=0):
        return self.n + d if self.reg is None else self.reg * self.per + (self.n + d)

    def begin(self, reg, per):
        self.reg, self.per, self.n0 = reg, per, self.n

    def end(self, turns):
        assert self.n - self.n0 == self.per, (self.n - self.n0, self.per)
        self.n, self.reg = self.n0 + self.per * turns, None


def build(nc, x_in, ctx_kT, ctx_v, g_x, g_f, w_qkvT, w_projT, b_proj, router_w, w1, w2, bias, out):
    stack = ExitStack()
    phase1 = ExitStack()
    phase2 = ExitStack()

    def sb(name, shape, dt, where=stack):
        return where.enter_context(nc.sbuf_tensor(name, shape, dt))

    def sem(name):
        return stack.enter_context(nc.semaphore(name))

    with stack:
        ident = sb("ident", [P, P], F32)
        below = sb("below", [P, P], BF16)
        ones = sb("ones", [P, P], BF16)
        iota_e = sb("iota_e", [P, E], F32)
        slot_base = sb("slot_base", [P, TOPK, E], F32)
        token_no = sb("token_no", [P, B * QT], F32)
        gates = sb("gates", [P, 2], F32)
        tanh_g = sb("tanh_g", [P, 2], F32)
        b_row = sb("b_row", [P, C], F32)
        bias_row = sb("bias_row", [P, C], F32)
        x_sb = sb("x_sb", [P, B * QT, C], F32)
        w1_raw = [sb("w1_raw0", [P, 2, F], F32)]
        w2_raw = [sb("w2_raw0", [P, F // P, C], F32)]
        stats = sb("stats", [P, B * QT, 6], F32)
        meanvar = sb("meanvar", [P, B * QT, 2], F32)
        rstd = sb("rstd", [P, B * QT], F32)
        var = sb("var", [P, B * QT], F32)
        held_p = sb("held_p", [P, 10], F32)
        held = sb("held", [P, 2], F32)
        root_t = sb("root_t", [P, B * QT], F32)

        k6 = sb("k6", [P, H, NKEY], BF16, phase1)
        q6 = sb("q6", [P, H, T], BF16, phase1)
        v_stash = sb("v_stash", [P, 2, B, QT, C], F32, phase1)
        v_ones = sb("v_ones", [P, KT, H, 2 * D], F32, phase1)
        o_t = sb("o_t", [P, T], F32, phase1)
        o_nat = sb("o_nat", [P, QT, C], F32, phase1)
        o_natT = sb("o_natT", [P, 2, T], F32, phase1)
        w_p = sb("w_p", [P, 2, C], F32, phase1)
        w_r = sb("w_r", [P, 2, EW], F32, phase1)
        lgT = sb("logits_T", [P, P], F32, phase1)
        xd = sb("xd", [P, QT, ROW], F32, phase1)
        x1T = sb("x1T", [P, 2, T], F32, phase1)
        shift = sb("shift", [P, QT], F32, phase1)
        rden = sb("rden", [P, QT, HG], F32, phase1)
        mx = sb("mx", [P, 2, SLOTS_PER_GROUP], F32, phase1)
        neg_m = sb("neg_m", [SLOTS_PER_GROUP, P], F32, phase1)
        neg_parts = sb("neg_parts", [SLOTS_PER_GROUP, NPART, P], BF16, phase1)
        lmax = sb("lmax", [P, QT], F32, phase1)
        lshift = sb("lshift", [P, QT, E], F32, phase1)
        lexp = sb("lexp", [P, QT, E], F32, phase1)
        lsum = sb("lsum", [P, QT], F32, phase1)
        score = sb("score", [P, QT, E], F32, phase1)
        top = sb("top", [P, QT, 8], F32, phase1)
        top_e = sb("top_e", [P, QT, 8], U32, phase1)
        top_ef = sb("top_ef", [P, QT, TOPK], F32, phase1)
        hot = sb("hot", [P, QT, TOPK * E], BF16, phase1)
        hot_sum = sb("hot_sum", [P, TOPK * E], F32, phase1)
        carry = sb("carry", [P, TOPK * E], BF16, phase1)
        pos = sb("pos", [P, QT, TOPK * E], F32, phase1)
        over = sb("over", [P, QT, TOPK * E], F32, phase1)
        slot_f = sb("slot_f", [P, QT, TOPK], F32, phase1)
        slot_u = sb("slot_u", [P, QT, TOPK], U32, phase1)
        with ExitStack() as early:
            prj = sb("prj", [P, 2, T], F32, early)
        parts = sb("parts", [P, NPART, 4, T], BF16, phase1)
        c_parts = sb("c_parts", [P, NPART, 2, T], BF16, phase1)
        empty = sb("empty", [P, ROW], F32, phase1)
        with ExitStack() as early:
            xn = sb("xn", [P, QT, C], F32, early)
            xnT = sb("xnT", [P, 2, T], F32, early)
            w_qkv = sb("w_qkv", [P, 2, 3 * C], F32, early)
            sb("to_third", [P, HG * T - 6 * C], F32, early)
            ctxk = sb("ctxk", [P, 2, T], F32, early)
            sb("to_fourth", [P, 2, T], F32, early)
            qk = sb("qk", [P, 4, T], F32, early)
        pexp = [sb(f"pexp{i}", [P, HG, T], F32, phase1) for i in range(NP)]
        phase1.close()

        w1_p = [[sb(f"w1_{h}0", [P, 2, F], F32R, phase2) for h in ("hi", "lo")]]
        w2_p = [[sb(f"w2_{h}0", [P, F // P, C], F32R, phase2) for h in ("hi", "lo")]]
        w1_raw.append(sb("w1_raw1", [P, 2, F], F32, phase2))
        w2_raw.append(sb("w2_raw1", [P, F // P, C], F32, phase2))
        xe = [sb(f"xe{i}", [P, SLOTS // P, ROW], F32, phase2) for i in range(2)]
        tok_u = [sb(f"tok_u{i}", [P, SLOTS // P], U32, phase2) for i in range(2)]
        xeT = [sb(f"xeT_{h}", [P, 2, SLOTS], F32R, phase2) for h in ("hi", "lo")]
        w1_p.append([sb(f"w1_{h}1", [P, 2, F], F32R, phase2) for h in ("hi", "lo")])
        w2_p.append([sb(f"w2_{h}1", [P, F // P, C], F32R, phase2) for h in ("hi", "lo")])
        hid = sb("hid", [P, 4, SLOTS], F32, phase2)
        hid_p = [sb(f"hid_{h}", [P, F // P, SLOTS], F32R, phase2) for h in ("hi", "lo")]
        y_sb = [sb(f"y_sb{i}", [P, SLOTS // P, C], F32, phase2) for i in range(2)]
        phase2.close()

        ps = stack.enter_context(nc.psum_tensor("ps", [P, 8, 512], F32))

        q_dram = nc.dram_tensor("q_parts", (B, NPART, C, T), BF16, kind="Internal").ap()
        k_dram = nc.dram_tensor("k_parts", (B, NPART, C, NKEY), BF16, kind="Internal").ap()
        slot_dram = nc.dram_tensor("slot_rows", (NSLOT, ROW), F32, kind="Internal").ap()

        chain_v, chain_p = sem("chain_v"), sem("chain_p")
        x0_in = sem("x0_loaded")
        consts_in, x_in_s, w_in, vctx_in, ctxk_in = (sem(n) for n in (
            "consts_in", "x_loaded", "w_loaded", "vctx_loaded", "ctxk_loaded"))
        gate_in, gates_done = sem("gates_loaded"), sem("gates_done")
        consts_done, empty_done, empty_out = sem("consts_done"), sem("empty_done"), sem("empty_out")
        xn_done, xnT_ready, xnT_done = sem("xn_done"), sem("xnT_ready"), sem("xnT_done")
        qkv_ready, qkv_out = sem("qkv_ready"), sem("qkv_out")
        high_done, middle_done = sem("q_high_done"), sem("q_middle_done")
        parts_done, cparts_done = [sem("q_parts_done"), sem("k_parts_done")], sem("cparts_done")
        parts_out, cparts_out = [sem("q_parts_stored"), sem("k_parts_stored")], sem("cparts_stored")
        xb_done = sem("xb_done")
        one_row, k_ones = sem("one_row"), sem("k_ones")
        qk_in = [sem(f"qk_loaded{g}") for g in range(G)]
        shift_in = [sem(f"shift_in{g}") for g in range(G)]
        s_ready, max_done = sem("max_scores_ready"), sem("max_done")
        st_ready, exp_done = sem("scores_ready"), sem("exp_done")
        pv_done, o_copied = sem("pv_done"), sem("o_copied")
        v_set = sem("v_set")
        misc_ready, misc_free = sem("misc_ready"), sem("misc_free")
        shift_done = sem("shift_parts_done")
        x1_done, xd_done = sem("x1_done"), sem("xd_done")
        root_done, x1_added = sem("root_done"), sem("x1_added")
        last_ready, x1T_done = sem("last_ready"), sem("x1T_done")
        lexp_done, hot_done, slot_done = sem("lexp_done"), sem("hot_done"), sem("slot_done")
        res_done, res_out = sem("residual_done"), sem("residual_stored")
        scattered = [sem("first_choices_scattered"), sem("second_choices_scattered")]
        first_in, first_ready, first_done = sem("first_half_in"), sem("first_ready"), sem("first_done")
        w_raw_in = [sem(f"w_raw_in{i}") for i in range(2)]
        xe_in = [sem(f"xe_in{i}") for i in range(2)]
        xeT_ready, xeT_done = sem("xeT_ready"), sem("xeT_done")
        w_hi, w1_lo, w2_lo = sem("w_hi"), sem("w1_lo"), sem("w2_lo")
        h_ready, h_out, hid_done = sem("h_ready"), sem("h_out"), sem("hid_done")
        hhi_done, y_ready, y_done = sem("hhi_done"), sem("y_ready"), sem("y_done")
        tok_done, added, rows_added = sem("tok_done"), sem("added"), sem("rows_added")
        xd_free = sem("xd_free")

        def bank(i, n=1):
            return ps[:, i, :] if n == 1 else ps[:, i:i + n, :]

        def pieces(x):
            flat = x[:, :, :].rearrange("p a b -> p (a b)")
            return [flat[:, 0:F], flat[:, F:2 * F]]

        def scores_bank(c, j):
            return bank(j if c > STEPS - LEAD and c % 2 else 4 + j)

        MISC = bank(7)
        SPE = SLOTS // P
        FT = F // P

        def run_steps(eng, steps, tallies, turn=TURN):
            steps(0, turn)
            with eng.Fori(0, B - 1) as i:
                for t, per in tallies:
                    t.begin(i, per)
                steps(turn, turn + PERIOD, i)
                for t, per in tallies:
                    t.end(B - 1)
            steps(turn + PERIOD * (B - 1), STEPS + PERIOD)

        block = stack.enter_context(nc.Block())

        @block.sync
        def _(sp):
            st, shifts = Tally(), Tally()

            def load_ctxk(b):
                sp.wait_ge(cparts_done, b + 1)
                sp.dma_start(ctxk[:, :, :], ctx_kT[b].rearrange("(m p) t -> p m t", p=P)).then_inc(ctxk_in, 16)

            def store_ctx(b):
                sp.wait_ge(cparts_done, b + 2)
                for i in range(NPART):
                    sp.dma_start(k_dram[b, i, :, 0:TC].rearrange("(m p) t -> p m t", p=P),
                                 c_parts[:, i, :, :]).then_inc(cparts_out, 16)
                if b + 1 < B:
                    load_ctxk(b + 1)

            def store_qk(b):
                for half, dram in enumerate((q_dram[b], k_dram[b, :, :, TC:NKEY])):
                    sp.wait_ge(parts_done[half], b + 2)
                    for i in range(NPART):
                        sp.dma_start(dram[i].rearrange("(m p) t -> p m t", p=P),
                                     parts[:, i, 2 * half:2 * half + 2, :]).then_inc(parts_out[half], 16)

            def wait_stored(b):
                sp.wait_ge(cparts_out, 3 * 16 * (b + 2))
                for half in range(2):
                    sp.wait_ge(parts_out[half], 3 * 16 * (b + 2))

            def fill_slots(piece):
                n = NSLOT // P // 4
                sp.wait_ge(empty_done, 1)
                sp.dma_start(slot_dram.rearrange("(n p) c -> p n c", p=P)[:, piece * n:(piece + 1) * n, :],
                             empty[:, :].rearrange("p (o c) -> p o c", o=1).to_broadcast([P, n, ROW])) \
                    .then_inc(empty_out, 16)

            def shift_rows(g):
                sp.wait_ge(shift_done, shifts.at())
                for i in range(NPART):
                    sp.dma_start(q6[KROWS + i:KROWS + i + 1, HG * g:HG * (g + 1), :]
                                 .rearrange("o h (q t) -> o (h q) t", t=P),
                                 neg_parts[:, i, :]).then_inc(shift_in[g], 16)

            def load_weights(e, k):
                sp.dma_start(w1_raw[k][:, :, :], w1[bass.ds(e, 1)].rearrange("a (k p) f -> p (a k) f", p=P)) \
                    .then_inc(w_raw_in[k], 16)
                sp.dma_start(w2_raw[k][:, :, :], w2[bass.ds(e, 1)].rearrange("a (k p) c -> p (a k) c", p=P)) \
                    .then_inc(w_raw_in[k], 16)

            def load_rows(e, k):
                sp.dma_start(xe[k][:, :, :], slot_dram[bass.ds(e * SLOTS, SLOTS), :]
                             .rearrange("(s p) c -> p s c", p=P)).then_inc(xe_in[k], 16)

            def load_group(b, g):
                for r, (pq, pk) in enumerate(PAIRS):
                    sp.dma_start(q6[r * D:(r + 1) * D, HG * g:HG * (g + 1), :],
                                 q_dram[bass.ds(b, 1), pq, HG * D * g:HG * D * (g + 1), :]
                                 .rearrange("a (h d) t -> d (a h) t", d=D)).then_inc(qk_in[g], 16)
                    sp.dma_start(k6[r * D:(r + 1) * D, HG * g:HG * (g + 1), :],
                                 k_dram[bass.ds(b, 1), pk, HG * D * g:HG * D * (g + 1), :]
                                 .rearrange("a (h d) t -> d (a h) t", d=D)).then_inc(qk_in[g], 16)

            for half in range(2):
                sp.sem_inc(parts_out[half], 3 * 16)
            sp.dma_start(x_sb[:, 0:QT, :], x_in[0:T, :].rearrange("(t p) c -> p t c", p=P)).then_inc(x0_in, 16)
            sp.dma_start(w_qkv[:, :, :], w_qkvT.rearrange("(k p) n -> p k n", p=P)).then_inc(w_in, 16)
            load_ctxk(0)
            sp.dma_start(gates[:, 0:1], g_x.broadcast_to([P, 1])).then_inc(gate_in, 16)
            sp.dma_start(gates[:, 1:2], g_f.broadcast_to([P, 1])).then_inc(gate_in, 16)
            sp.dma_start(x_sb[:, QT:, :], x_in[T:, :].rearrange("(t p) c -> p t c", p=P)).then_inc(x_in_s, 16)
            sp.wait_ge(one_row, 1)
            sp.dma_start(k6[KROWS:AROWS, 1:H, :], k6[KROWS:AROWS, 0:1, :].to_broadcast([NPART, H - 1, NKEY])) \
                .then_inc(k_ones, 16)
            sp.dma_start(b_row[:, :], b_proj.broadcast_to([P, C])).then_inc(consts_in, 16)
            sp.dma_start(bias_row[:, :], bias.broadcast_to([P, C])).then_inc(consts_in, 16)
            sp.dma_start(w_p[:, :, :], w_projT.rearrange("(k p) n -> p k n", p=P)).then_inc(consts_in, 16)
            sp.wait_ge(empty_done, 1)
            sp.dma_start(w_r[:, :, 0:E], router_w.rearrange("(k p) n -> p k n", p=P)).then_inc(consts_in, 16)
            sp.dma_start(v_stash[:, 0, :, :, :].rearrange("p b t c -> p (b t) c"),
                         ctx_v.rearrange("b (t p) c -> p (b t) c", p=P)).then_inc(vctx_in, 16)
            store_ctx(0)
            fill_slots(0)
            fill_slots(1)
            store_qk(0)
            wait_stored(0)
            load_group(0, 0)
            store_ctx(1)
            store_qk(1)
            load_group(0, 1)
            store_ctx(2)
            load_group(0, 2)
            store_qk(2)
            load_group(0, 3)
            store_ctx(3)
            shifts.step()
            shift_rows(0)
            store_qk(3)
            fill_slots(2)
            fill_slots(3)
            wait_stored(B - 1)
            load_weights(0, 0)

            def steps(c0, c1, i=0):
                for c in range(c0, c1):
                    for what, n in steps_at(c):
                        if what == "scores":
                            st.step(2)
                        elif what == "load":
                            sp.wait_ge(st_ready, st.at(-4))
                            load_group(i + n // G, n % G)
                        elif what == "turn_max":
                            shifts.step()
                            shift_rows(n % G)

            run_steps(sp, steps, [(st, 2 * PERIOD), (shifts, G)], turn=2)

            sp.wait_ge(st_ready, 2 * STEPS)
            load_weights(1, 1)
            sp.wait_ge(pv_done, NGROUP * KT)
            for k, done in enumerate((first_in, xe_in[0])):
                sp.wait_ge(scattered[k], B * QT * 16)
                sp.dma_start(xe[0][:, 2 * k:2 * k + 2, :],
                             slot_dram[k * CAP:(k + 1) * CAP, :].rearrange("(s p) c -> p s c", p=P)).then_inc(done, 16)
            load_rows(1, 1)

            def reload(n, k):
                sp.wait_ge(w1_lo, n * 2 + 2)
                sp.wait_ge(w2_lo, n * 2 + 2)
                load_weights(n + 2, k)
                sp.wait_ge(y_done, (n + 1) * SPE + 2)
                load_rows(n + 2, k)

            with sp.Fori(0, (E - 2) // 2) as j:
                reload(j * 2, 0)
                reload(j * 2 + 1, 1)
            sp.wait_ge(added, E * SPE * 16)

        @block.gpsimd
        def _(pool):
            link_n = Tally()

            def link(ins):
                ins.then_inc(chain_p, 1)
                link_n.step()
                pool.wait_ge(chain_p, link_n.at())

            def touch(k):
                return pool.tensor_tensor(held_p[:, k:k + 1], held_p[:, 9:10], held_p[:, 9:10], ALU.mult)

            def hold(k):
                touch(k).then_inc(chain_p, 1)
                link_n.step()

            def copy(dst, src):
                names = {2: "p (a) -> p a", 3: "p (a b) -> p a b", 4: "p (a b c) -> p a b c"}[len(src.shape)]
                units = {k: 1 for k in "abc"[:len(src.shape) - 2]}
                one = held_p[0:src.shape[0], 9:10].rearrange(names, **units)
                return pool.tensor_tensor(dst, src, one.to_broadcast(list(src.shape)), ALU.mult)

            def spread(row, n):
                return row[:, :].rearrange("p (o c) -> p o c", o=1).to_broadcast([P, n, C])

            pool.sem_inc(cparts_done, 1)
            pool.sem_inc(cparts_out, 3 * 16)
            pool.sem_inc(xd_free, 1)
            pool.sem_inc(rows_added, 2)
            link(pool.memset(held_p[:, 9:10], 1.0))
            link(pool.memset(ident[:, :], 0.0))
            pool.affine_select(out=ident[:, :], in_=ident[:, :], compare_op=ALU.not_equal, fill=1.0, base=0,
                               pattern=[[-1, P]], channel_multiplier=1).then_inc(consts_done, 1)

            link(pool.memset(ones[:, :], 1.0))
            pool.affine_select(out=below[:, :], in_=ones[:, :], compare_op=ALU.is_gt, fill=0.0, base=0,
                               pattern=[[1, P]], channel_multiplier=-1)
            pool.iota(iota_e[:, :], pattern=[[1, E]], base=0, channel_multiplier=0,
                      allow_small_or_imprecise_dtypes=True)
            pool.iota(slot_base[:, :, :], pattern=[[CAP, TOPK], [SLOTS, E]], base=0, channel_multiplier=0,
                      allow_small_or_imprecise_dtypes=True)
            pool.iota(token_no[:, :], pattern=[[P, B * QT]], base=0, channel_multiplier=1,
                      allow_small_or_imprecise_dtypes=True)
            pool.memset(carry[:, :], 0.0)
            pool.memset(w_r[:, :, :], 0.0)
            link(pool.memset(empty[:, :], 0.0))
            pool.memset(empty[:, C + TOPK:ROW], float(NOBODY)).then_inc(empty_done, 1)

            def batch(b):
                pool.wait_ge(ctxk_in, (b + 1) * 16)
                pool.wait_ge(cparts_out, (b + 1) * (3 * 16))
                link(copy(c_parts[:, 0], ctxk[:, :, :]))
                link(pool.tensor_tensor(ctxk[:, :, :], ctxk[:, :, :], c_parts[:, 0], ALU.subtract))
                link(copy(c_parts[:, 1], ctxk[:, :, :]))
                pool.tensor_tensor(c_parts[:, 2], ctxk[:, :, :], c_parts[:, 1], ALU.subtract) \
                    .then_inc(cparts_done, 1)

            pv, turn, rt = Tally(), Tally(), Tally()

            def set_v(b, g):
                for half in range(2):
                    ins = copy(
                        v_ones[:, half * QT:(half + 1) * QT, HG * g:HG * (g + 1), 0:D],
                        v_stash[:, half, bass.ds(b, 1), :, HG * D * g:HG * D * (g + 1)]
                        .rearrange("p o t (h d) -> p (o t) h d", d=D))
                ins.then_inc(v_set, 1)

            def cut_max():
                pool.wait_ge(misc_free, turn.at())
                link(copy(neg_parts[:, 0, :], neg_m[:, :]))
                link(pool.tensor_tensor(neg_m[:, :], neg_m[:, :], neg_parts[:, 0, :], ALU.subtract))
                link(copy(neg_parts[:, 1, :], neg_m[:, :]))
                pool.tensor_tensor(neg_parts[:, 2, :], neg_m[:, :], neg_parts[:, 1, :], ALU.subtract) \
                    .then_inc(shift_done, 1)

            def last_part(b):
                pool.wait_ge(middle_done, b + 1)
                pool.tensor_tensor(parts[:, 2, 0:2, :], qk[:, 0:2, :], parts[:, 1, 0:2, :], ALU.subtract) \
                    .then_inc(parts_done[0], 1)

            with pool.Fori(0, B - 1) as b:
                link_n.begin(b, 3)
                batch(b)
                last_part(b)
                link_n.end(B - 1)
            pool.memset(v_ones[:, :, :, D:2 * D], 1.0).then_inc(consts_done, 1)
            pool.wait_ge(vctx_in, 16)
            pool.wait_ge(qkv_out, 6 + 2)
            for g in range(G):
                set_v(0, g)
            batch(B - 1)
            last_part(B - 1)
            pool.wait_ge(qkv_out, 6 * B + 2)
            turn.step()
            cut_max()
            pool.wait_ge(gates_done, 1)
            pool.wait_ge(consts_in, 4 * 16)
            pool.tensor_scalar(bias_row[:, :], bias_row[:, :], tanh_g[:, 1:2], None, ALU.mult)
            link(pool.tensor_scalar(b_row[:, :], b_row[:, :], tanh_g[:, 0:1], None, ALU.mult))
            pool.wait_ge(xn_done, B)
            pool.tensor_tensor(x_sb[:, :, :], x_sb[:, :, :], spread(b_row, B * QT), ALU.add).then_inc(xb_done, 1)

            def cut_w1(n, k):
                for j, (lo, raw, hi) in enumerate(zip(pieces(w1_p[k][1]), pieces(w1_raw[k]), pieces(w1_p[k][0]))):
                    pool.wait_ge(w_hi, n * 4 + (j + 1))
                    pool.tensor_tensor(lo, raw, hi, ALU.subtract).then_inc(w1_lo, 1)

            def steps(c0, c1, i=0):
                for c in range(c0, c1):
                    for what, n in steps_at(c):
                        if what in SHARED:
                            turn.step()
                        if what == "norm1" and c >= STEPS:
                            cut_w1(0, 0)
                        if what in ("proj0", "proj1"):
                            half = int(what[-1])
                            rows = x_sb[:, bass.ds((i + n) * QT + 2 * half, 2), :].rearrange("p o c -> p (o c)")
                            pool.wait_ge(xb_done, 1)
                            pool.wait_ge(misc_free, turn.at())
                            hold(3 + half)
                            pool.tensor_tensor(rows, rows, prj[:, half, :], ALU.add).then_inc(x1_added, 1)
                        if what == "values":
                            pv.step()
                        elif what == "set_v":
                            pool.wait_ge(pv_done, pv.at(-1 - 2 * KT))
                            set_v(i + n // G, n % G)
                        elif what == "turn_max":
                            pool.wait_ge(shift_in[(n - 1) % G], (i + ((n - 1) // G + 1)) * (16 * NPART))
                            cut_max()
                        elif what == "scatter":
                            rt.step()
                            pool.wait_ge(empty_out, 4 * 16)
                            pool.wait_ge(slot_done, rt.at())
                            hold(0)
                            for k in range(TOPK):
                                for t in range(QT):
                                    pool.indirect_dma_start(
                                        out=slot_dram, out_offset=bass.IndirectOffsetOnAxis(
                                            ap=slot_u[:, t, k:k + 1], axis=0),
                                        in_=xd[:, t, :], in_offset=None,
                                        bounds_check=NSLOT - 1, oob_is_err=False).then_inc(scattered[k], 16)
                            pool.wait_ge(xd_done, rt.at())
                            hold(5)
                            rows = x_sb[:, bass.ds(i * QT + n * QT, QT), :]
                            pool.tensor_tensor(rows, rows, spread(bias_row, QT), ALU.add).then_inc(res_done, 1)
                            pool.wait_ge(res_done, rt.at())
                            hold(1)
                            pool.dma_start(out[bass.ds(i * T + n * T, T), :].rearrange("(q p) c -> p q c", p=P),
                                           rows).then_inc(res_out, 16)
                            for k in range(TOPK):
                                pool.wait_ge(scattered[k], rt.at() * (QT * 16))
                            touch(2).then_inc(xd_free, 1)

            run_steps(pool, steps, [(pv, G * KT), (turn, TURNS), (rt, 1), (link_n, 3 * G + 5)])

            def add_rows(n, k):
                pool.wait_ge(tok_done, n + 1)
                link(touch(8))
                for s in range(SPE):
                    pool.wait_ge(y_done, n * SPE + (s + 3))
                    hold(3 + s)
                    pool.indirect_dma_start(
                        out=out, out_offset=bass.IndirectOffsetOnAxis(ap=tok_u[k][:, s:s + 1], axis=0),
                        in_=y_sb[k][:, s, :], in_offset=None, bounds_check=NTOK - 1, oob_is_err=False,
                        compute_op=ALU.add).then_inc(added, 16)
                pool.wait_ge(added, n * (SPE * 16) + SPE * 16)
                touch(7).then_inc(rows_added, 1)

            pool.wait_ge(res_out, B * 16)
            with pool.Fori(0, (E - 2) // 2) as j:
                link_n.begin(j, 2 * (SPE + 1))
                cut_w1(j * 2 + 1, 1)
                add_rows(j * 2, 0)
                cut_w1(j * 2 + 2, 0)
                add_rows(j * 2 + 1, 1)
                link_n.end((E - 2) // 2)
            cut_w1(E - 1, 1)
            add_rows(E - 2, 0)
            add_rows(E - 1, 1)

        @block.scalar
        def _(act):
            act.sem_inc(qkv_out, 6)
            act.sem_inc(h_out, 4)
            act.wait_ge(gate_in, 32)
            act.activation(tanh_g[:, :], gates[:, :], ACT.Tanh).then_inc(gates_done, 1)
            st, kt_n, turn, oc, rt, tmax = (Tally() for _ in range(6))

            def evict(dst, scale=1.0, src=MISC):
                turn.step()
                act.wait_ge(misc_ready, turn.at())
                return act.activation(dst, src, ACT.Identity, scale=scale).then_inc(misc_free, 1)

            def cut_high(n, k):
                act.wait_ge(w_raw_in[k], (n - k) * 16 + 32)
                for raw, part in ((w1_raw, w1_p), (w2_raw, w2_p)):
                    for hi, src in zip(pieces(part[k][0]), pieces(raw[k])):
                        act.activation(hi, src, ACT.Copy).then_inc(w_hi, 1)

            def turn_max():
                tmax.step()
                evict(neg_m[:, :], -1.0, MISC[0:SLOTS_PER_GROUP, 0:P])

            def project(b, last=False):
                for k in range(2):
                    act.wait_ge(xnT_ready, b * 2 + (k + 1))
                    act.activation(xnT[:, k, :], bank(6 + k), ACT.Copy).then_inc(xnT_done, 1)
                for j in range(2):
                    act.wait_ge(qkv_ready, b * 6 + (j + 1))
                    act.activation(v_stash[:, 1, bass.ds(b, 1), 2 * j:2 * j + 2, :].rearrange("p o t c -> p (o t c)"),
                                   bank(6 + j), ACT.Copy).then_inc(qkv_out, 1)
                for m in range(4):
                    if m % 2 == 0:
                        act.wait_ge(parts_done[m // 2], b + 1)
                        act.wait_ge(parts_out[m // 2], (b + 1) * (3 * 16))
                    act.wait_ge(qkv_ready, b * 6 + (m + 3))
                    scale = D ** -0.5 if m < 2 else 1.0
                    act.activation(qk[:, m, :], bank(4 + m % 2), ACT.Copy, scale=scale)
                    act.activation(parts[:, 0, m, :], bank(4 + m % 2), ACT.Copy, scale=scale).then_inc(qkv_out, 1)
                    if m == 2:
                        act.wait_ge(high_done, b + 1)
                        act.activation(parts[:, 1, 0:2, :], qk[:, 0:2, :], ACT.Copy).then_inc(middle_done, 1)
                        if last:
                            turn_max()

            with act.Fori(0, B - 1) as b:
                project(b)
            project(B - 1, last=True)

            def steps(c0, c1, i=0):
                for c in range(c0, c1):
                    for what, n in steps_at(c):
                        if what == "scores":
                            kt, pair = c % SLOTS_PER_GROUP // 2, c % 2
                            buf = pexp[kt % NP]
                            if pair == 0:
                                kt_n.step()
                                if c == 4:
                                    act.wait_ge(cparts_done, B + 1)
                                if c == 6:
                                    act.wait_ge(parts_done[0], B + 1)
                                    act.wait_ge(parts_done[1], B + 1)
                                if c >= 2 * NP:
                                    act.wait_ge(pv_done, kt_n.at(-NP))
                            for j in range(2):
                                st.step()
                                act.wait_ge(st_ready, st.at())
                                act.activation(buf[:, 2 * pair + j, :], scores_bank(c, j), ACT.Exp).then_inc(exp_done, 1)
                        elif what == "copy_out":
                            oc.step()
                            act.wait_ge(pv_done, oc.at() * KT)
                            act.wait_ge(misc_ready, turn.at())
                            act.activation(o_t[:, :], bank(6), ACT.Copy).then_inc(o_copied, 1)
                        elif what == "turn_max":
                            act.wait_ge(shift_done, tmax.at())
                            turn_max()
                        elif what in ("attn_t0", "attn_t1"):
                            evict(o_natT[:, int(what[-1]), :])
                        elif what in ("last_t0", "last_t1"):
                            evict(o_natT[:, int(what[-1]), :])
                        elif what in ("x1_t0", "x1_t1"):
                            evict(x1T[:, int(what[-1]), :])
                        elif what in ("proj0", "proj1"):
                            evict(prj[:, int(what[-1]), :], scale=tanh_g[:, 0:1])
                        elif what == "norm0" and c >= STEPS:
                            act.wait_ge(root_done, 1)
                            act.wait_ge(xd_free, B)
                            for t in (0, 1):
                                ins = act.activation(xd[:, t, 0:C], x_sb[:, n * QT + t, :], ACT.Identity,
                                                     bias=shift[:, t:t + 1], scale=rstd[:, t:t + 1])
                            ins.then_inc(x1_done, 1)
                        elif what == "router":
                            evict(lgT[:, :], src=MISC[:, 0:P])
                        elif what == "last_x1_t":
                            act.wait_ge(last_ready, 3)
                            act.activation(x1T[:, 0, :], bank(4), ACT.Copy).then_inc(x1T_done, 1)
                        elif what in SHARED:
                            turn.step()
                        elif what == "softmax":
                            rt.step()
                            act.wait_ge(misc_free, turn.at())
                            act.activation(lexp[:, :, :], lshift[:, :, :], ACT.Exp).then_inc(lexp_done, 1)
                        if what == "last_t1":
                            cut_high(0, 0)

            run_steps(act, steps, [(st, 2 * PERIOD), (kt_n, G * KT), (turn, TURNS), (oc, G), (rt, 1), (tmax, G)])

            def hidden(n):
                for f in range(FT):
                    act.wait_ge(h_ready, n * FT + (f + 1))
                    act.wait_ge(hid_done, n * FT + (f + 1))
                    act.activation(hid[:, f % 4, :], bank(2 + f % 4), ACT.Gelu_apprx_tanh).then_inc(h_out, 1)
                    act.wait_ge(h_out, n * FT + (f + 5))
                    act.activation(hid_p[0][:, f, :], hid[:, f % 4, :], ACT.Copy).then_inc(hhi_done, 1)

            hidden(0)
            with act.Fori(0, (E - 2) // 2) as j:
                cut_high(j * 2 + 1, 1)
                hidden(j * 2 + 1)
                cut_high(j * 2 + 2, 0)
                hidden(j * 2 + 2)
            cut_high(E - 1, 1)
            hidden(E - 1)

        @block.vector
        def _(dve):
            link_n = Tally()

            def link(ins):
                ins.then_inc(chain_v, 1)
                link_n.step()
                dve.wait_ge(chain_v, link_n.at())

            def hold():
                dve.tensor_copy(held[:, 0:1], held[:, 1:2]).then_inc(chain_v, 1)
                link_n.step()

            def x_row(b, t):
                return x_sb[:, bass.ds(b * QT + t, 1), :].rearrange("p o c -> p (o c)")

            def moments(slots, row):
                for t in slots:
                    ins = dve.bn_stats(stats[:, t, :], row(t))
                return ins

            def variance(slots):
                hold()
                for t in slots:
                    ins = dve.bn_aggr(meanvar[:, t, :], stats[:, t, :])
                link(ins)
                at = slice(slots[0], slots[-1] + 1)
                link(dve.tensor_scalar(var[:, at], meanvar[:, at, 1], EPS, None, ALU.add))
                link(dve.tensor_scalar(rstd[:, at].bitcast(I32), var[:, at].bitcast(I32), -0.5, ROOT_SEED,
                                       ALU.mult, ALU.add))

            def newton(slots):
                at = slice(slots[0], slots[-1] + 1)
                link(dve.scalar_tensor_tensor(out=root_t[:, at], in0=rstd[:, at], scalar=-0.5, in1=rstd[:, at],
                                              op0=ALU.mult, op1=ALU.mult))
                link(dve.tensor_tensor(root_t[:, at], root_t[:, at], var[:, at], ALU.mult))
                link(dve.scalar_tensor_tensor(out=rstd[:, at], in0=root_t[:, at], scalar=1.5, in1=rstd[:, at],
                                              op0=ALU.add, op1=ALU.mult))

            def normalise(dst, b, tiles, slot=0):
                for t in tiles:
                    ins = dve.tensor_scalar(dst[:, t, 0:C], x_row(b, t), meanvar[:, slot + t, 0:1],
                                            rstd[:, slot + t:slot + t + 1], ALU.subtract, ALU.mult)
                return ins

            def norms_of(slots):
                link(moments(slots, lambda t: x_sb[:, t, :]))
                variance(slots)
                for _ in range(NEWTON):
                    newton(slots)

            def cut_q(b):
                dve.wait_ge(qkv_out, b * 6 + 10)
                dve.tensor_tensor(qk[:, 0:2, :], qk[:, 0:2, :], parts[:, 0, 0:2, :], ALU.subtract) \
                    .then_inc(high_done, 1)

            def cut_k(b):
                dve.wait_ge(qkv_out, b * 6 + 12)
                x = qk[:, 2:4, :]
                link(dve.tensor_tensor(x, x, parts[:, 0, 2:4, :], ALU.subtract))
                link(dve.tensor_copy(parts[:, 1, 2:4, :], x))
                dve.tensor_tensor(parts[:, 2, 2:4, :], x, parts[:, 1, 2:4, :], ALU.subtract) \
                    .then_inc(parts_done[1], 1)

            unit, turn, rt, xa = (Tally() for _ in range(4))

            def row_max(u):
                unit.step()
                dve.wait_ge(s_ready, unit.at())
                group, j = u // SLOTS_PER_GROUP, u % SLOTS_PER_GROUP
                dve.reduce_max(mx[:, group % 2, j:j + 1], bank(2 * (u % 2), 2).rearrange("p a t -> p (a t)"),
                               AX_X).then_inc(max_done, 1)

            def normalise_next(b):
                for t in range(QT):
                    slot = b * QT + t
                    ins = dve.tensor_scalar(xn[:, t, :], x_row(b, t), at_slot(meanvar[:, :, 0], slot),
                                            at_slot(rstd, slot), ALU.subtract, ALU.mult)
                ins.then_inc(xn_done, 1)

            def at_slot(x, slot):
                return x[:, bass.ds(slot, 1)]

            def next_batch(b):
                dve.wait_ge(xnT_ready, (b + 1) * 2)
                normalise_next(b + 1)

            for half in range(2):
                dve.sem_inc(parts_done[half], 1)
            dve.sem_inc(hid_done, 4)
            dve.sem_inc(y_done, 2)
            dve.memset(k6[KROWS:P, 0:1, :], 1.0).then_inc(one_row, 1)
            link(dve.memset(held[:, :], 0.0))
            dve.wait_ge(x0_in, 16)
            hold()
            norms_of(range(QT))
            normalise(xn, 0, range(QT)).then_inc(xn_done, 1)
            dve.wait_ge(x_in_s, 16)
            hold()
            norms_of(range(QT, B * QT))
            with dve.Fori(0, B - 2) as b:
                link_n.begin(b, 2)
                next_batch(b)
                cut_q(b)
                cut_k(b)
                link_n.end(B - 2)
            for b, counts in UNITS_AFTER.items():
                if b + 1 < B:
                    next_batch(b)
                for point, count in enumerate(counts):
                    for _ in range(count):
                        row_max(unit.n)
                    if point == 2:
                        cut_q(b)
                cut_k(b)

            def wait_turn():
                turn.step()
                dve.wait_ge(misc_ready, turn.at())

            def per_row(x, n, shape):
                return x.rearrange("p (q o) -> p q o", o=1).to_broadcast(shape)

            def steps(c0, c1, i=0):
                for c in range(c0, c1):
                    for what, n in steps_at(c):
                        if what == "max":
                            row_max(n)
                        elif what == "turn_out":
                            wait_turn()
                            o4 = MISC.rearrange("p (q h d) -> p q h d", q=QT, h=HG)
                            link(dve.reciprocal(rden[:, :, :], o4[:, :, :, D]))
                            g = n % G
                            dve.tensor_tensor(
                                o_nat[:, :, HG * D * g:HG * D * (g + 1)].rearrange("p q (h d) -> p q h d", d=D),
                                o4[:, :, :, 0:D],
                                rden[:, :, :].rearrange("p q (h o) -> p q h o", o=1).to_broadcast([P, QT, HG, D]),
                                ALU.mult).then_inc(misc_free, 1)
                        elif what == "last_proj1":
                            for j in range(2):
                                rows = x_sb[:, n * QT + 2 * j:n * QT + 2 * j + 2, :]
                                dve.wait_ge(last_ready, j + 1)
                                link(dve.scalar_tensor_tensor(out=rows, in0=bank(2 - 2 * j, 2)[:, :, 0:C], scalar=tanh_g[:, 0:1], in1=rows,
                                                              op0=ALU.mult, op1=ALU.add))
                                hold()
                                ins = moments(range(2 * j, 2 * j + 2), lambda t: x_row(n, t))
                            link(ins)
                        elif what == "last_x1_t":
                            dve.wait_ge(last_ready, 4)
                            dve.tensor_copy(x1T[:, 1, :], bank(5)).then_inc(x1T_done, 1)
                            cut_w2(0, 0, 0)
                            cut_w2(0, 0, 1)
                        elif what in ("stats0", "stats1"):
                            xa.step()
                            dve.wait_ge(x1_added, xa.at())
                            hold()
                            half = int(what[-1])
                            link(moments(range(2 * half, 2 * half + 2), lambda t: x_row(i + n, t)))
                        elif what == "variance":
                            variance(range(QT))
                        elif what == "newton":
                            newton(range(QT))
                        elif what == "norm0":
                            rt.step()
                            dve.wait_ge(xd_free, rt.at())
                            if c < STEPS:
                                normalise(xd, i + n, (0, 1))
                            else:
                                dve.scalar_tensor_tensor(out=shift[:, :], in0=meanvar[:, 0:QT, 0], scalar=-1.0,
                                                         in1=rstd[:, 0:QT], op0=ALU.mult, op1=ALU.mult) \
                                    .then_inc(root_done, 1)
                        elif what == "norm1":
                            normalise(xd, i + n, (2, 3)).then_inc(x1_done, 1)
                        elif what == "router_t":
                            wait_turn()
                            lg = MISC[:, 0:P].rearrange("p (q e) -> p q e", e=EW)[:, :, 0:E]
                            link(dve.tensor_reduce(lmax[:, :], lg, AX_X, ALU.max))
                            dve.tensor_tensor(lshift[:, :, :], lg, per_row(lmax[:, :], E, [P, QT, E]),
                                              ALU.subtract).then_inc(misc_free, 1)
                        elif what == "top2":
                            dve.wait_ge(lexp_done, rt.at())
                            link(dve.tensor_reduce(lsum[:, :], lexp[:, :, :], AX_X, ALU.add))
                            link(dve.reciprocal(lsum[:, :], lsum[:, :]))
                            link(dve.tensor_tensor(score[:, :, :], lexp[:, :, :],
                                                   per_row(lsum[:, :], E, [P, QT, E]), ALU.mult))
                            hold()
                            for t in range(QT):
                                ins = dve.max(top[:, t, :], score[:, t, :])
                            link(ins)
                        elif what == "expert_of":
                            hold()
                            for t in range(QT):
                                ins = dve.max_index(top_e[:, t, :], top[:, t, :], score[:, t, :])
                            link(ins)
                            link(dve.tensor_copy(top_ef[:, :, :], top_e[:, :, 0:TOPK]))
                            for k in range(TOPK):
                                ins = dve.tensor_tensor(
                                    hot[:, :, k * E:(k + 1) * E],
                                    iota_e[:, :].rearrange("p (o e) -> p o e", o=1).to_broadcast([P, QT, E]),
                                    per_row(top_ef[:, :, k], E, [P, QT, E]), ALU.is_equal)
                            ins.then_inc(hot_done, 1)
                            dve.tensor_scalar(xd[:, :, C:C + TOPK], top[:, :, 0:TOPK], tanh_g[:, 1:2], None, ALU.mult)
                            dve.tensor_copy(xd[:, :, C + TOPK:ROW].rearrange("p q o -> p (q o)"),
                                            token_no[:, bass.ds((i + n) * QT, QT)]).then_inc(xd_done, 1)
                        elif what == "ranks":
                            wait_turn()
                            rk = MISC[:, 0:QT * TOPK * E].rearrange("p (q n) -> p q n", n=TOPK * E)
                            base = slot_base[:, :, :].rearrange("p (o k) e -> p o (k e)", o=1) \
                                .to_broadcast([P, QT, TOPK * E])
                            dve.tensor_tensor(pos[:, :, :], rk, base, ALU.add)
                            dve.tensor_scalar(over[:, :, :], rk, float(CAP), float(DROPPED), ALU.is_ge, ALU.mult) \
                                .then_inc(misc_free, 1)
                            link(dve.tensor_reduce(hot_sum[:, :], hot[:, :, :].rearrange("p q n -> p n q"),
                                                   AX_X, ALU.add))
                            dve.wait_ge(misc_free, turn.at())
                            dve.tensor_tensor(carry[:, :], carry[:, :], hot_sum[:, :], ALU.add)
                            link(dve.tensor_tensor(pos[:, :, :], pos[:, :, :], over[:, :, :], ALU.add))
                            link(dve.tensor_tensor(pos[:, :, :], pos[:, :, :], hot[:, :, :], ALU.mult))
                            link(dve.tensor_reduce(slot_f[:, :, :], pos[:, :, :].rearrange("p q (k e) -> p q k e", e=E),
                                                   AX_X, ALU.add))
                            dve.tensor_copy(slot_u[:, :, :], slot_f[:, :, :]).then_inc(slot_done, 1)
                        elif what in SHARED:
                            turn.step()

            def cut_w2(n, k, j):
                dve.wait_ge(w_hi, n * 4 + (j + 3))
                dve.tensor_tensor(pieces(w2_p[k][1])[j], pieces(w2_raw[k])[j], pieces(w2_p[k][0])[j],
                                  ALU.subtract).then_inc(w2_lo, 1)

            turn.step()
            run_steps(dve, steps, [(unit, PERIOD), (turn, TURNS), (rt, 1), (xa, 2),
                                   (link_n, G + NORM_LINKS + 1 + 8 + 4)])

            def cut_rows(n, k, halves=False):
                if halves:
                    for h in range(2):
                        for c in range(2):
                            at, src = slice(h * CAP, (h + 1) * CAP), bank(2 * h + c)[:, 0:CAP]
                            dve.wait_ge(first_ready, 2 * h + c + 1)
                            link(dve.tensor_copy(xeT[0][:, c, at], src))
                            dve.tensor_tensor(xeT[1][:, c, at], src, xeT[0][:, c, at], ALU.subtract) \
                                .then_inc(first_done, 1)
                    dve.sem_inc(xeT_done, 2)
                else:
                    for c in range(2):
                        dve.wait_ge(xeT_ready, n * 2 + (c + 1))
                        link(dve.tensor_copy(xeT[0][:, c, :], bank(c)))
                        dve.tensor_tensor(xeT[1][:, c, :], bank(c), xeT[0][:, c, :], ALU.subtract) \
                            .then_inc(xeT_done, 1)
                dve.wait_ge(rows_added, n + 1)
                dve.tensor_copy(tok_u[k][:, :], xe[k][:, :, ROW - 1]).then_inc(tok_done, 1)

            def results(n, k):
                for s in range(SPE):
                    dve.wait_ge(y_ready, n * SPE + (s + 1))
                    w = C + s * P // CAP
                    dve.tensor_scalar(y_sb[k][:, s, :], bank(6 + s % 2)[:, 0:C], xe[k][:, s, w:w + 1], None,
                                      ALU.mult).then_inc(y_done, 1)

            def hidden(n, k, first=False):
                for f in range(FT):
                    dve.wait_ge(hhi_done, n * FT + (f + 1))
                    dve.tensor_tensor(hid_p[1][:, f, :], hid[:, f % 4, :], hid_p[0][:, f, :], ALU.subtract) \
                        .then_inc(hid_done, 1)
                    if f in (1, 3) and not first:
                        cut_w2(n, k, f // 2)

            cut_rows(0, 0, halves=True)
            hidden(0, 0, first=True)

            def expert(n, k):
                cut_rows(n, k)
                results(n - 1, 1 - k)
                hidden(n, k)

            with dve.Fori(0, (E - 2) // 2) as j:
                link_n.begin(j, 4)
                expert(j * 2 + 1, 1)
                expert(j * 2 + 2, 0)
                link_n.end((E - 2) // 2)
            expert(E - 1, 1)
            results(E - 1, 1)

        @block.tensor
        def _(pe):
            pe.wait_ge(w_in, 16)
            pe.wait_ge(consts_done, 1)
            unit, st, pv, turn, group, rt = (Tally() for _ in range(6))

            def max_scores(u, i=0):
                g, j = u // SLOTS_PER_GROUP, u % SLOTS_PER_GROUP
                head, qt = g % G * HG + j // QT, j % QT
                if j == 0:
                    pe.wait_ge(qk_in[g % G], (i + (g // G + 1)) * (2 * 16 * len(PAIRS)))
                if u >= 2:
                    pe.wait_ge(max_done, unit.at(-1))
                for half in range(2):
                    mm = pe.matmul(bank(2 * (u % 2) + half), q6[0:KROWS, head, qt * P:(qt + 1) * P],
                                   k6[0:KROWS, head, half * 512:(half + 1) * 512], start=True, stop=True)
                mm.then_inc(s_ready, 1)
                unit.step()

            def take_turn(u=None):
                if u is None:
                    pe.wait_ge(misc_free, turn.at())
                turn.step()

            def turn_max(g, first=False):
                pe.wait_ge(max_done, group_units(g))
                take_turn(0 if first else None)
                pe.transpose(MISC[0:SLOTS_PER_GROUP, 0:P], mx[:, g % 2, :], ident[:, :]).then_inc(misc_ready, 1)

            tm = Tally()

            def group_units(g):
                tm.step()
                return tm.at() * SLOTS_PER_GROUP

            def project(b, counts=()):
                def units(point):
                    if counts:
                        for _ in range(counts[point]):
                            max_scores(unit.n)

                pe.wait_ge(xn_done, b + 1)
                pe.wait_ge(qkv_out, b * 6 + 2)
                for k in range(2):
                    for t in range(QT):
                        mm = pe.transpose(bank(6 + k)[:, t * P:(t + 1) * P], xn[:, t, k * P:(k + 1) * P], ident[:, :])
                    mm.then_inc(xnT_ready, 1)
                pe.wait_ge(xnT_done, b * 2 + 2)
                for j in range(2):
                    for t in range(2):
                        for k in range(2):
                            mm = pe.matmul(bank(6 + j)[:, t * C:(t + 1) * C],
                                           xnT[:, k, (2 * j + t) * P:(2 * j + t + 1) * P], w_qkv[:, k, 2 * C:3 * C],
                                           start=(k == 0), stop=(k == 1))
                    mm.then_inc(qkv_ready, 1)
                units(0)
                for m in range(4):
                    pe.wait_ge(qkv_out, b * 6 + (5 + m + 2 * (m // 2)))
                    for k in range(2):
                        mm = pe.matmul(bank(4 + m % 2), w_qkv[:, k, m * P:(m + 1) * P], xnT[:, k, :],
                                       start=(k == 0), stop=(k == 1))
                    mm.then_inc(qkv_ready, 1)
                    units(m + 1)
                    if m == 2 and len(counts) and b == B - 1:
                        turn_max(0, first=True)

            with pe.Fori(0, B - 2) as b:
                project(b)
            pe.wait_ge(k_ones, 16)
            for b, counts in UNITS_AFTER.items():
                project(b, counts)
            pe.wait_ge(qkv_out, 6 * (B + 1))

            def steps(c0, c1, i=0):
                for c in range(c0, c1):
                    s = c % SLOTS_PER_GROUP
                    for what, n in steps_at(c):
                        if what == "max":
                            max_scores(n, i)
                        elif what == "scores":
                            g, kt, pair = c // SLOTS_PER_GROUP, s // 2, s % 2
                            if s == 0:
                                pe.wait_ge(shift_in[g % G], (i + (g // G + 1)) * (16 * NPART))
                            for j in range(2):
                                head = g % G * HG + 2 * pair + j
                                if c == STEPS - LEAD + 1 and j == 0:
                                    pe.wait_ge(max_done, STEPS)
                                elif c >= STEPS - LEAD + 2:
                                    pe.wait_ge(exp_done, st.at(-3))
                                elif 1 <= c <= STEPS - LEAD:
                                    pe.wait_ge(exp_done, st.at(-1))
                                pe.matmul(scores_bank(c, j), k6[0:AROWS, head, kt * P:(kt + 1) * P], q6[0:AROWS, head, :],
                                          start=True, stop=True).then_inc(st_ready, 1)
                                st.step()
                        elif what == "values":
                            g = (c - (3 if c > STEPS - LEAD else 1)) // SLOTS_PER_GROUP
                            if n == 0:
                                group.step()
                                pe.wait_ge(v_set, group.at())
                                if c >= SLOTS_PER_GROUP:
                                    pe.wait_ge(o_copied, group.at(-1))
                            pv.step()
                            pe.wait_ge(exp_done, pv.at() * HG)
                            for j in range(HG):
                                mm = pe.matmul(bank(6)[j * 2 * D:(j + 1) * 2 * D, :],
                                               v_ones[:, n, g % G * HG + j, :], pexp[n % NP][:, j, :],
                                               start=(n == 0), stop=(n == KT - 1))
                            mm.then_inc(pv_done, 1)
                        elif what == "turn_out":
                            pe.wait_ge(o_copied, group.at(to_out(c)))
                            take_turn()
                            for q in range(QT):
                                mm = pe.transpose(MISC[:, q * P:(q + 1) * P], o_t[:, q * P:(q + 1) * P], ident[:, :])
                            mm.then_inc(misc_ready, 1)
                        elif what == "turn_max":
                            turn_max(n)
                        elif what in ("attn_t0", "attn_t1", "x1_t0", "x1_t1"):
                            k = int(what[-1])
                            take_turn()
                            if what == "attn_t0":
                                rt.step()
                            if what == "x1_t0":
                                pe.wait_ge(x1_done, rt.at())
                            src = o_nat if what[0] == "a" else xd
                            for q in range(QT):
                                mm = pe.transpose(MISC[:, q * P:(q + 1) * P], src[:, q, k * P:(k + 1) * P], ident[:, :])
                            mm.then_inc(misc_ready, 1)
                        elif what in ("proj0", "proj1"):
                            j = int(what[-1])
                            take_turn()
                            pe.wait_ge(consts_in, 4 * 16)
                            for t in range(2):
                                for k in range(2):
                                    mm = pe.matmul(MISC[:, t * C:(t + 1) * C],
                                                   o_natT[:, k, (2 * j + t) * P:(2 * j + t + 1) * P], w_p[:, k, :],
                                                   start=(k == 0), stop=(k == 1))
                            mm.then_inc(misc_ready, 1)
                        elif what in ("last_t0", "last_t1"):
                            k = int(what[-1])
                            take_turn()
                            if k:
                                rt.step()
                            for q in range(QT):
                                mm = pe.transpose(MISC[:, q * P:(q + 1) * P], o_nat[:, q, k * P:(k + 1) * P],
                                                  ident[:, :])
                            mm.then_inc(misc_ready, 1)
                        elif what in ("last_proj0", "last_proj_2", "last_proj_3", "last_proj1"):
                            if what in ("last_proj0", "last_proj1"):
                                pe.wait_ge(misc_free, turn.at())
                                pe.wait_ge(consts_in, 4 * 16)
                            else:
                                pe.wait_ge(exp_done, 2 * STEPS)
                            half = int(what == "last_proj1")
                            tiles = {"last_proj0": (0, 1), "last_proj1": range(QT)}.get(what, (int(what[-1]),))
                            for t in tiles:
                                mm = pe.matmul(bank((2 + t) % QT)[:, 0:C], o_natT[:, half, t * P:(t + 1) * P],
                                               w_p[:, half, :], start=(half == 0), stop=(half == 1))
                                if half and t % 2:
                                    mm.then_inc(last_ready, 1)
                        elif what == "last_x1_t":
                            pe.wait_ge(x1_done, rt.at(1))
                            for k in range(2):
                                for q in range(QT):
                                    mm = pe.transpose(bank(4 + k)[:, q * P:(q + 1) * P], xd[:, q, k * P:(k + 1) * P],
                                                      ident[:, :])
                                mm.then_inc(last_ready, 1)
                        elif what == "router":
                            take_turn()
                            if c >= STEPS:
                                pe.wait_ge(x1T_done, 2)
                            for k in range(2):
                                for t in range(QT):
                                    mm = pe.matmul(MISC[t * EW:(t + 1) * EW, 0:P], w_r[:, k, :],
                                                   x1T[:, k, t * P:(t + 1) * P], start=(k == 0), stop=(k == 1))
                            mm.then_inc(misc_ready, 1)
                        elif what == "router_t":
                            take_turn()
                            pe.transpose(MISC[:, 0:P], lgT[:, :], ident[:, :]).then_inc(misc_ready, 1)
                        elif what == "ranks":
                            take_turn()
                            pe.wait_ge(hot_done, rt.at())
                            n16 = TOPK * E
                            for t in range(QT):
                                dst = MISC[:, t * n16:(t + 1) * n16]
                                pe.matmul(dst, below[:, :], hot[:, t, :], start=True, stop=False)
                                for before in range(t):
                                    pe.matmul(dst, ones[:, :], hot[:, before, :], start=False, stop=False)
                                mm = pe.matmul(dst, ones[:, :], carry[:, :], start=False, stop=True)
                            mm.then_inc(misc_ready, 1)

            def to_out(c):
                return -1 if c < STEPS else 0

            run_steps(pe, steps, [(unit, PERIOD), (st, 2 * PERIOD), (pv, G * KT), (turn, TURNS), (group, G),
                                  (rt, 1), (tm, G)])

            def first_rows():
                for h, came in enumerate((first_in, xe_in[0])):
                    pe.wait_ge(came, 16)
                    for c in range(2):
                        for s in range(2):
                            mm = pe.transpose(bank(2 * h + c)[:, s * P:(s + 1) * P],
                                              xe[0][:, 2 * h + s, c * P:(c + 1) * P], ident[:, :])
                        mm.then_inc(first_ready, 1)
                pe.sem_inc(xeT_ready, 2)

            def rows(n, k):
                pe.wait_ge(xe_in[k], (n - k) * 8 + 16)
                for c in range(2):
                    for s in range(SPE):
                        mm = pe.transpose(bank(c)[:, s * P:(s + 1) * P], xe[k][:, s, c * P:(c + 1) * P], ident[:, :])
                    mm.then_inc(xeT_ready, 1)

            PASSES = [(0, 0), (0, 1), (1, 0)]

            def hidden(n, k, first=False):
                pe.wait_ge(w1_lo, n * 2 + 2)
                for f in range(FT):
                    pe.wait_ge(h_out, n * FT + (f + 1))
                    terms = [(c, a, b) for c in range(2) for a, b in PASSES]
                    for c, a, b in terms:
                        if f == 0 and (a, b) == PASSES[0]:
                            if first:
                                pe.wait_ge(first_done, 3 + c)
                            else:
                                pe.wait_ge(xeT_done, n * 2 + (c + 1))
                        mm = pe.matmul(bank(2 + f % 4), w1_p[k][a][:, c, f * P:(f + 1) * P], xeT[b][:, c, :],
                                       start=(c, a, b) == terms[0], stop=(c, a, b) == terms[-1])
                    mm.then_inc(h_ready, 1)

            def results(n, k):
                pe.wait_ge(w2_lo, n * 2 + 2)
                for s in range(SPE):
                    pe.wait_ge(y_done, n * SPE + (s + 1))
                    terms = [(f, a, b) for f in range(FT) for a, b in PASSES]
                    for f, a, b in terms:
                        if s == 0 and (a, b) == PASSES[0]:
                            pe.wait_ge(hid_done, n * FT + (f + 5))
                        mm = pe.matmul(bank(6 + s % 2)[:, 0:C], hid_p[a][:, f, s * P:(s + 1) * P], w2_p[k][b][:, f, :],
                                       start=(f, a, b) == terms[0], stop=(f, a, b) == terms[-1])
                    mm.then_inc(y_ready, 1)

            first_rows()
            hidden(0, 0, first=True)
            with pe.Fori(0, (E - 2) // 2) as j:
                rows(j * 2 + 1, 1)
                results(j * 2, 0)
                hidden(j * 2 + 1, 1)
                rows(j * 2 + 2, 0)
                results(j * 2 + 1, 1)
                hidden(j * 2 + 2, 0)
            rows(E - 1, 1)
            results(E - 2, 0)
            hidden(E - 1, 1)
            results(E - 1, 1)


_OUT = ((B, T, C), "float32")


def kernel(**inputs):
    import concourse.bacc as _bacc
    import numpy as _np
    from concourse.bass_utils import run_bass_kernel_spmd as _run

    a = {k: _np.asarray(v) for k, v in inputs.items()}
    ctx = a["ctx_2048"]
    arrays = {
        "x": a["x"].reshape(NTOK, C),
        "ctx_kT": ctx[:, :, 0:C].transpose(0, 2, 1),
        "ctx_v": ctx[:, :, C:2 * C],
        "g_xattn": a["g_xattn"].reshape(1, 1),
        "g_ffn": a["g_ffn"].reshape(1, 1),
        "w_qkvT": a["L0_xattn_w_qkv"].T,
        "w_projT": a["L0_xattn_w_proj"].T,
        "b_proj": a["L0_xattn_b_proj"].reshape(1, C),
        "router_w": a["L0_ffn_router_w"],
        "w1": a["L0_ffn_w1"],
        "w2": a["L0_ffn_w2"],
        "bias": a["L0_ffn_bias"].reshape(1, C),
    }
    arrays = {k: _np.ascontiguousarray(v) for k, v in arrays.items()}
    nc = _bacc.Bacc("TRN2", target_bir_lowering=False, num_devices=1)
    args = [nc.dram_tensor(k, v.shape, mybir.dt.from_np(v.dtype), kind="ExternalInput").ap()
            for k, v in arrays.items()]
    args.append(nc.dram_tensor("out", (NTOK, C), F32, kind="ExternalOutput").ap())
    build(nc, *args)
    r = _run(nc, [arrays], core_ids=[0])
    return r.results[0]["out"].reshape(_OUT[0])
```
